# Optimizing a Trainium2 kernel written in Bass

```python
import numpy as np
import jax
import jax.numpy as jnp

def _softmax(x, axis=-1):
    return jax.nn.softmax(x, axis=axis)

def _gelu(x):
    return jax.nn.gelu(x, approximate=True)

def _silu(x):
    return jax.nn.silu(x)

def _sigmoid(x):
    return jax.nn.sigmoid(x)

def _layernorm(x, axis=-1, eps=1e-05):
    m = jnp.mean(x, axis=axis, keepdims=True)
    v = jnp.var(x, axis=axis, keepdims=True)
    return (x - m) / jnp.sqrt(v + eps)

def _scatter_add(tgt, idx, src, axis=0):
    return tgt.at[idx].add(src)

def _segment_sum(src, seg, n):
    return jax.ops.segment_sum(src, seg, n)
kernel_name = 'mk_dlrm_tower_d1_rec_r8_8f63c8'

def setup_inputs(seed: int=0):
    np.random.seed(seed)
    _w = jnp.asarray

    def _rec_inputs():
        import jax
        import jax.numpy as jnp
        _tk = jax.random.key(seed)
        ids = jnp.stack([jax.random.randint(jax.random.fold_in(_tk, 200 + f), (2048,), 0, v, jnp.int32) for f, v in enumerate([1250, 1000, 1250, 12500, 1250, 1000, 125000, 1000, 1250, 1000, 12500, 1250, 1250, 1250, 1250, 1250, 1250, 1000, 1250, 1250, 1000, 1250, 1000, 12500, 1000, 1000])], axis=1)
        tbl_0 = 0.05 * jax.random.normal(jax.random.fold_in(_tk, 500 + 0), (1250, 128), jnp.float32)
        tbl_1 = 0.05 * jax.random.normal(jax.random.fold_in(_tk, 500 + 1), (1000, 128), jnp.float32)
        tbl_2 = 0.05 * jax.random.normal(jax.random.fold_in(_tk, 500 + 2), (1250, 128), jnp.float32)
        tbl_3 = 0.05 * jax.random.normal(jax.random.fold_in(_tk, 500 + 3), (12500, 128), jnp.float32)
        tbl_4 = 0.05 * jax.random.normal(jax.random.fold_in(_tk, 500 + 4), (1250, 128), jnp.float32)
        tbl_5 = 0.05 * jax.random.normal(jax.random.fold_in(_tk, 500 + 5), (1000, 128), jnp.float32)
        tbl_6 = 0.05 * jax.random.normal(jax.random.fold_in(_tk, 500 + 6), (125000, 128), jnp.float32)
        tbl_7 = 0.05 * jax.random.normal(jax.random.fold_in(_tk, 500 + 7), (1000, 128), jnp.float32)
        tbl_8 = 0.05 * jax.random.normal(jax.random.fold_in(_tk, 500 + 8), (1250, 128), jnp.float32)
        tbl_9 = 0.05 * jax.random.normal(jax.random.fold_in(_tk, 500 + 9), (1000, 128), jnp.float32)
        tbl_10 = 0.05 * jax.random.normal(jax.random.fold_in(_tk, 500 + 10), (12500, 128), jnp.float32)
        tbl_11 = 0.05 * jax.random.normal(jax.random.fold_in(_tk, 500 + 11), (1250, 128), jnp.float32)
        tbl_12 = 0.05 * jax.random.normal(jax.random.fold_in(_tk, 500 + 12), (1250, 128), jnp.float32)
        tbl_13 = 0.05 * jax.random.normal(jax.random.fold_in(_tk, 500 + 13), (1250, 128), jnp.float32)
        tbl_14 = 0.05 * jax.random.normal(jax.random.fold_in(_tk, 500 + 14), (1250, 128), jnp.float32)
        tbl_15 = 0.05 * jax.random.normal(jax.random.fold_in(_tk, 500 + 15), (1250, 128), jnp.float32)
        tbl_16 = 0.05 * jax.random.normal(jax.random.fold_in(_tk, 500 + 16), (1250, 128), jnp.float32)
        tbl_17 = 0.05 * jax.random.normal(jax.random.fold_in(_tk, 500 + 17), (1000, 128), jnp.float32)
        tbl_18 = 0.05 * jax.random.normal(jax.random.fold_in(_tk, 500 + 18), (1250, 128), jnp.float32)
        tbl_19 = 0.05 * jax.random.normal(jax.random.fold_in(_tk, 500 + 19), (1250, 128), jnp.float32)
        tbl_20 = 0.05 * jax.random.normal(jax.random.fold_in(_tk, 500 + 20), (1000, 128), jnp.float32)
        tbl_21 = 0.05 * jax.random.normal(jax.random.fold_in(_tk, 500 + 21), (1250, 128), jnp.float32)
        tbl_22 = 0.05 * jax.random.normal(jax.random.fold_in(_tk, 500 + 22), (1000, 128), jnp.float32)
        tbl_23 = 0.05 * jax.random.normal(jax.random.fold_in(_tk, 500 + 23), (12500, 128), jnp.float32)
        tbl_24 = 0.05 * jax.random.normal(jax.random.fold_in(_tk, 500 + 24), (1000, 128), jnp.float32)
        tbl_25 = 0.05 * jax.random.normal(jax.random.fold_in(_tk, 500 + 25), (1000, 128), jnp.float32)
        _rk = jax.random.fold_in(_tk, 7)
        r_dense_features = -0.000520686 + 1.00062 * jax.random.normal(jax.random.fold_in(_rk, 101), (2048, 128), jnp.float32)
        W_top1 = 0.0405887 * jax.random.normal(jax.random.fold_in(_tk, 801), (607, 512), jnp.float32)
        W_top2 = 0.0441942 * jax.random.normal(jax.random.fold_in(_tk, 802), (512, 256), jnp.float32)
        W_top3 = 0.0625 * jax.random.normal(jax.random.fold_in(_tk, 803), (256, 1), jnp.float32)
        b_top1 = jnp.zeros((512,), jnp.float32)
        b_top2 = jnp.zeros((256,), jnp.float32)
        return (r_dense_features, ids, tbl_0, tbl_1, tbl_2, tbl_3, tbl_4, tbl_5, tbl_6, tbl_7, tbl_8, tbl_9, tbl_10, tbl_11, tbl_12, tbl_13, tbl_14, tbl_15, tbl_16, tbl_17, tbl_18, tbl_19, tbl_20, tbl_21, tbl_22, tbl_23, tbl_24, tbl_25, W_top1, b_top1, W_top2, b_top2, W_top3)
    r_dense_features, ids, tbl_0, tbl_1, tbl_2, tbl_3, tbl_4, tbl_5, tbl_6, tbl_7, tbl_8, tbl_9, tbl_10, tbl_11, tbl_12, tbl_13, tbl_14, tbl_15, tbl_16, tbl_17, tbl_18, tbl_19, tbl_20, tbl_21, tbl_22, tbl_23, tbl_24, tbl_25, W_top1, b_top1, W_top2, b_top2, W_top3 = _rec_inputs()

    def _L0_rec_setup():
        import jax, jax.numpy as jnp
        import numpy as np
        F = 26
        B, D = (2048, 128)
        _IU0, _IU1 = np.triu_indices(F + 1, k=1)
        _IU0 = jnp.asarray(_IU0)
        _IU1 = jnp.asarray(_IU1)
        key = jax.random.key(seed)
        k1, k2 = jax.random.split(key)
        dense_features = jax.random.normal(k1, (B, D), dtype=jnp.float32)
        sparse_features = jax.random.normal(k2, (B, F, D), dtype=jnp.float32)
        return {'dense_features': dense_features, 'sparse_features': sparse_features}
    _L0_rec_all = _L0_rec_setup()
    _L0_rec_in = {k: v for k, v in _L0_rec_all.items() if k in ()}
    del _L0_rec_all
    return {'r_dense_features': r_dense_features, 'ids': ids, 'tbl_0': tbl_0, 'tbl_1': tbl_1, 'tbl_2': tbl_2, 'tbl_3': tbl_3, 'tbl_4': tbl_4, 'tbl_5': tbl_5, 'tbl_6': tbl_6, 'tbl_7': tbl_7, 'tbl_8': tbl_8, 'tbl_9': tbl_9, 'tbl_10': tbl_10, 'tbl_11': tbl_11, 'tbl_12': tbl_12, 'tbl_13': tbl_13, 'tbl_14': tbl_14, 'tbl_15': tbl_15, 'tbl_16': tbl_16, 'tbl_17': tbl_17, 'tbl_18': tbl_18, 'tbl_19': tbl_19, 'tbl_20': tbl_20, 'tbl_21': tbl_21, 'tbl_22': tbl_22, 'tbl_23': tbl_23, 'tbl_24': tbl_24, 'tbl_25': tbl_25, 'W_top1': W_top1, 'b_top1': b_top1, 'W_top2': W_top2, 'b_top2': b_top2, 'W_top3': W_top3}

def reference(r_dense_features, ids, tbl_0, tbl_1, tbl_2, tbl_3, tbl_4, tbl_5, tbl_6, tbl_7, tbl_8, tbl_9, tbl_10, tbl_11, tbl_12, tbl_13, tbl_14, tbl_15, tbl_16, tbl_17, tbl_18, tbl_19, tbl_20, tbl_21, tbl_22, tbl_23, tbl_24, tbl_25, W_top1, b_top1, W_top2, b_top2, W_top3):
    import jax
    import jax.numpy as jnp

    def _L0_rec_ref(dense_features, sparse_features):
        import jax, jax.numpy as jnp
        import numpy as np
        F = 26
        B, D = (2048, 128)
        _IU0, _IU1 = np.triu_indices(F + 1, k=1)
        _IU0 = jnp.asarray(_IU0)
        _IU1 = jnp.asarray(_IU1)
        combined = jnp.concatenate([dense_features[:, None, :], sparse_features], axis=1)
        interactions = jnp.einsum('bfd,bgd->bfg', combined, combined)
        interactions_flat = interactions[:, _IU0, _IU1]
        return jnp.concatenate([dense_features, interactions_flat], axis=1)
    e = jnp.stack([tbl_0[ids[:, 0]], tbl_1[ids[:, 1]], tbl_2[ids[:, 2]], tbl_3[ids[:, 3]], tbl_4[ids[:, 4]], tbl_5[ids[:, 5]], tbl_6[ids[:, 6]], tbl_7[ids[:, 7]], tbl_8[ids[:, 8]], tbl_9[ids[:, 9]], tbl_10[ids[:, 10]], tbl_11[ids[:, 11]], tbl_12[ids[:, 12]], tbl_13[ids[:, 13]], tbl_14[ids[:, 14]], tbl_15[ids[:, 15]], tbl_16[ids[:, 16]], tbl_17[ids[:, 17]], tbl_18[ids[:, 18]], tbl_19[ids[:, 19]], tbl_20[ids[:, 20]], tbl_21[ids[:, 21]], tbl_22[ids[:, 22]], tbl_23[ids[:, 23]], tbl_24[ids[:, 24]], tbl_25[ids[:, 25]]], axis=1)
    z = _L0_rec_ref(r_dense_features, e)
    z = z.reshape(z.shape[0], -1)
    h = jnp.concatenate([z, r_dense_features], axis=1)
    h = jnp.maximum(h @ W_top1 + b_top1, 0.0)
    h = jnp.maximum(h @ W_top2 + b_top2, 0.0)
    y = h @ W_top3
    return y

_drawn_inputs = setup_inputs


def setup_inputs(seed=0):
    import zlib

    import numpy as np

    out = dict(_drawn_inputs(seed))
    spreads = {'b_top1': (0.0, 0.1), 'b_top2': (0.0, 0.1)}
    factors = {}
    for name, (base, spread) in spreads.items():
        noise = np.random.default_rng([zlib.crc32(name.encode()), seed]).standard_normal(out[name].shape)
        drawn = base * np.exp(spread * noise) if base else spread * noise
        out[name] = jnp.asarray(drawn.astype(out[name].dtype))
    for name, factor in factors.items():
        out[name] = (out[name] * factor).astype(out[name].dtype)
    return out
```

```python
from contextlib import ExitStack

import numpy as np

import concourse.bass as bass
from concourse import mybir

F32, F16, BF16, I32 = mybir.dt.float32, mybir.dt.float16, mybir.dt.bfloat16, mybir.dt.int32
ALU = mybir.AluOpType

P = 128
BATCH, D, FEATURES = 2048, 128, 26
TILES = BATCH // P
PER_BLOCK = 2
BLOCKS = TILES // PER_BLOCK
COLS = PER_BLOCK * P
VECTORS = FEATURES + 1
SLOTS = 32
HALF = (VECTORS - 1) // 2
PAIRS = VECTORS * HALF
H1, H2 = 512, 256

PRODUCT_FEATURES = [1, 5, 7, 9, 17, 20]
ROW_FEATURES = [f for f in range(FEATURES) if f not in PRODUCT_FEATURES]
N_ROW, N_PRODUCT = len(ROW_FEATURES), len(PRODUCT_FEATURES)
SLOT_VECTORS = [0] + [f + 1 for f in ROW_FEATURES] + [f + 1 for f in PRODUCT_FEATURES]
PRODUCT_SLOT = 1 + N_ROW
TABLE_ROWS = 1000
CHUNKS = -(-TABLE_ROWS // P)
FULL = TABLE_ROWS // P
REST = TABLE_ROWS - FULL * P
PARTS = 3
GROUPS = [list(range(a, min(a + 4, PRODUCT_SLOT))) for a in range(0, PRODUCT_SLOT, 4)]
N_GROUPS = len(GROUPS)
IN_QUAD = 4
QUADS = P // IN_QUAD
PER_BANK = 4
FILLS = QUADS // PER_BANK
SQUARE = IN_QUAD * VECTORS
WRAPPED = VECTORS + HALF
F_PER_K = P // HALF
K_PAIRS = F_PER_K * HALF
K_TILES = 1 + PAIRS // K_PAIRS
SCRATCH_STORES = 2 * IN_QUAD
HIDDEN_LOADS = K_TILES - 1


def pair_rows():
    at = {}
    for a in range(VECTORS):
        for b in range(a + 1, VECTORS):
            at[a, b] = D + len(at)
    rows = []
    for f in range(VECTORS):
        for k in range(1, HALF + 1):
            pair = SLOT_VECTORS[f], SLOT_VECTORS[(f + k) % VECTORS]
            rows.append(at[min(pair), max(pair)])
    return rows


def build(nc, dense, ids, tables, W1, b1, W2, b2, W3, y):
    with ExitStack() as ctx:
        def sb(name, shape, dt=F32):
            return ctx.enter_context(nc.sbuf_tensor(name, shape, dt))

        def sem(name):
            return ctx.enter_context(nc.semaphore(name))

        def bank(name):
            return ctx.enter_context(nc.psum_tensor(name, [P, 512], F32))

        all_ids = sb("all_ids", [P, TILES, FEATURES], I32)
        tile_ids = sb("tile_ids", [P, PER_BLOCK, FEATURES], I32)
        ids16 = sb("ids16", [P, TILES, FEATURES], F16)
        spread_ids = sb("spread_ids", [P, N_PRODUCT, BLOCKS, COLS], F16)
        rows = sb("rows", [P, PER_BLOCK, PRODUCT_SLOT, D])
        staged = sb("staged", [P, 2, CHUNKS, D])
        parts = sb("parts", [P, N_PRODUCT, PARTS, CHUNKS, D], BF16)
        one_hot = sb("one_hot", [P, 2, CHUNKS, COLS], BF16)
        chunk_row = sb("chunk_row", [P, CHUNKS])
        identity = sb("identity", [P, P])
        identity16 = sb("identity16", [P, P], F16)
        combined = sb("combined", [P, PER_BLOCK, P, SLOTS])
        dots = sb("dots", [P, SQUARE, PER_BLOCK * QUADS])
        hidden0 = sb("hidden0", [P, K_TILES, COLS])
        hidden1 = sb("hidden1", [P, H1 // P, COLS])
        hidden2 = sb("hidden2", [P, H2 // P, PER_BLOCK, P])
        w1 = sb("w1", [P, K_TILES, H1])
        w1_again = sb("w1_again", [P, H1])
        w2 = sb("w2", [P, H1 // P, H2])
        w3 = sb("w3", [P, H2 // P])
        bias1 = sb("bias1", [P, H1 // P])
        bias2 = sb("bias2", [P, H2 // P])
        y_sb = sb("y_sb", [P, TILES])
        scratch = nc.dram_tensor("scratch", (SLOTS, WRAPPED, IN_QUAD, PER_BLOCK * QUADS), F32)
        scratch = scratch.ap()
        scratch_rows = scratch.rearrange("f g j s -> (f g) (j s)")

        turned = [bank(f"turned{i}") for i in range(2)]
        dot_bank = [bank(f"dot_bank{i}") for i in range(2)]
        looked_up = [bank(f"looked_up{i}") for i in range(2)]
        mlp_bank = [bank(f"mlp_bank{i}") for i in range(2)]

        ids_loaded = sem("ids_loaded")
        weights_loaded = sem("weights_loaded")
        table_loaded = [sem(f"table_loaded{i}") for i in range(2)]
        table_split = sem("table_split")
        part_made = sem("part_made")
        rest_made = sem("rest_made")
        constants_ready = sem("constants_ready")
        constant_step = sem("constant_step")
        padding_ready = sem("padding_ready")
        ids16_ready = sem("ids16_ready")
        ids_spread = sem("ids_spread")
        ids_copied = sem("ids_copied")
        weights_folded = sem("weights_folded")
        tile_may_start = sem("tile_may_start")
        tile_ids_ready = sem("tile_ids_ready")
        gathered = [[sem(f"gathered{u}_{g}") for g in range(N_GROUPS)] for u in range(PER_BLOCK)]
        dense_loaded = [sem(f"dense_loaded{u}") for u in range(PER_BLOCK)]
        one_hot_ready = sem("one_hot_ready")
        product_done = sem("product_done")
        product_copied = sem("product_copied")
        turned_done = sem("turned_done")
        turned_copied = [sem(f"turned_copied{i}") for i in range(2)]
        dots_done = sem("dots_done")
        dots_copied = sem("dots_copied")
        scratch_stored = sem("scratch_stored")
        hidden_loaded = sem("hidden_loaded")
        layer_done = sem("layer_done")
        layer_copied = sem("layer_copied")
        y_stored = sem("y_stored")

        block = ctx.enter_context(nc.Block())

        TURNS = PER_BLOCK * N_GROUPS
        EVEN_TURNS = TURNS // 2
        DOT_FILLS = PER_BLOCK * FILLS
        LAYER1, LAYER2 = H1 // P, H2 // P
        LAYERS = LAYER1 + LAYER2 + 1

        ids_by_tile = ids.rearrange("(p t) f -> p t f", t=TILES)
        dense_by_tile = dense.rearrange("(p t) d -> p t d", t=TILES)

        def load_dense(sp, m, u):
            sp.dma_start(rows[:, u, 0:1, :],
                         dense_by_tile[:, bass.ds(m * PER_BLOCK + u, 1), :]).then_inc(dense_loaded[u], 16)

        @block.sync
        def _(sp):
            sp.dma_start(all_ids[:], ids_by_tile).then_inc(ids_loaded, 16)
            for u in range(PER_BLOCK):
                load_dense(sp, 0, u)
            for n, f in enumerate(PRODUCT_FEATURES):
                if n >= 2:
                    sp.wait_ge(table_split, n - 1)
                t = tables[f]
                sp.dma_start(staged[:, n % 2, 0:FULL, :],
                             t[0:FULL * P, :].rearrange("(c p) d -> p c d", p=P)).then_inc(table_loaded[n % 2], 16)
                sp.dma_start(staged[0:REST, n % 2, FULL, :], t[FULL * P:TABLE_ROWS, :]).then_inc(table_loaded[n % 2], 16)
                if n == 1:
                    sp.dma_start(w1[:, 0, :], W1[0:D, :]).then_inc(weights_loaded, 16)
                    sp.dma_start(w1_again[:, :], W1[D + PAIRS:D + PAIRS + D, :]).then_inc(weights_loaded, 16)
                    sp.dma_start(w1[0:K_PAIRS, 1:K_TILES, :],
                                 W1[D:D + PAIRS, :].rearrange("(k p) n -> p k n", p=K_PAIRS)).then_inc(weights_loaded, 16)
                    sp.dma_start(w2[:], W2.rearrange("(k p) n -> p k n", p=P)).then_inc(weights_loaded, 16)
                    with nc.allow_non_contiguous_dma(reason="a few hundred words of biases, once"):
                        sp.dma_start(w3[:], W3.rearrange("(k p) o -> p (k o)", p=P)).then_inc(weights_loaded, 16)
                        sp.dma_start(bias1[:], b1.rearrange("(k p) -> p k", p=P)).then_inc(weights_loaded, 16)
                        sp.dma_start(bias2[:], b2.rearrange("(k p) -> p k", p=P)).then_inc(weights_loaded, 16)

            def through_scratch(m, first):
                sp.wait_ge(dots_copied, (m + 1) * DOT_FILLS)
                if not first:
                    sp.wait_ge(hidden_loaded, m * HIDDEN_LOADS * 16)
                for j in range(IN_QUAD):
                    own = dots[SLOTS * j:SLOTS * (j + 1), VECTORS * j:VECTORS * (j + 1), :]
                    sp.dma_start(scratch[:, 0:VECTORS, j, :], own).then_inc(scratch_stored, 16)
                    sp.dma_start(scratch[:, VECTORS:WRAPPED, j, :], own[:, 0:HALF, :]).then_inc(scratch_stored, 16)
                sp.wait_ge(scratch_stored, (m + 1) * SCRATCH_STORES * 16)
                for k in range(HIDDEN_LOADS):
                    step = WRAPPED + 1
                    at = step * F_PER_K * k + 1
                    pairs = scratch_rows[at:at + step * F_PER_K, :].rearrange("(f k) s -> f k s", k=step)[:, 0:HALF, :]
                    sp.dma_start(hidden0[0:K_PAIRS, 1 + k, :], pairs).then_inc(hidden_loaded, 16)

            def next_dense(m):
                for u in range(PER_BLOCK):
                    sp.wait_ge(turned_done, m * TURNS + (u + 1) * N_GROUPS)
                    load_dense(sp, m + 1, u)

            next_dense(0)
            through_scratch(0, True)
            with sp.Fori(1, BLOCKS - 1) as m:
                next_dense(m)
                through_scratch(m, False)
            through_scratch(BLOCKS - 1, False)
            sp.wait_ge(layer_copied, BLOCKS * LAYERS)
            sp.dma_start(y.rearrange("(p t) o -> p (t o)", t=TILES), y_sb[:]).then_inc(y_stored, 16)
            sp.wait_ge(y_stored, 16)

        @block.gpsimd
        def _(pool):
            def gather_tile(m, u, first):
                if not first:
                    pool.wait_ge(turned_done, (m - 1) * TURNS + (u + 1) * N_GROUPS)
                    pool.sem_inc(tile_may_start, 1)
                nc.gpsimd.tensor_copy(tile_ids[:, u, :], all_ids[:, bass.ds(m * PER_BLOCK + u, 1), :].rearrange(
                    "p t f -> p (t f)")).then_inc(ids_copied, 1)
                pool.wait_ge(ids_copied, m * PER_BLOCK + u + 1)
                pool.sem_inc(tile_ids_ready, 1)
                for g, slots in enumerate(GROUPS):
                    for slot in slots:
                        if slot == 0:
                            continue
                        f = ROW_FEATURES[slot - 1]
                        nc.gpsimd.indirect_dma_start(
                            rows[:, u, slot, :], None, tables[f][:, :],
                            bass.IndirectOffsetOnAxis(ap=tile_ids[:, u, f:f + 1], axis=0)).then_inc(gathered[u][g], 16)

            nc.gpsimd.memset(identity[:], 0.0).then_inc(constant_step, 1)
            nc.gpsimd.iota(chunk_row[:], pattern=[[P, CHUNKS]], base=0, channel_multiplier=1,
                           allow_small_or_imprecise_dtypes=True).then_inc(constants_ready, 1)
            pool.wait_ge(constant_step, 1)
            nc.gpsimd.affine_select(out=identity[:], in_=identity[:], compare_op=ALU.not_equal, fill=1.0, base=0,
                                    pattern=[[-1, P]], channel_multiplier=1).then_inc(constants_ready, 1)
            pool.wait_ge(ids_loaded, 16)
            for u in range(PER_BLOCK):
                gather_tile(0, u, True)
            with pool.Fori(1, BLOCKS) as m:
                for u in range(PER_BLOCK):
                    gather_tile(m, u, False)

        @block.tensor
        def _(pe):
            pe.wait_ge(ids16_ready, 2)
            for n in range(N_PRODUCT):
                for t in range(0, TILES, 4):
                    i = n * (TILES // 4) + t // 4
                    if i >= 2:
                        pe.wait_ge(ids_spread, i - 1)
                    f = PRODUCT_FEATURES[n]
                    for q in range(4):
                        last = nc.tensor.matmul(looked_up[i % 2][:, q * P:(q + 1) * P],
                                                ids16[:, t + q, f:f + 1].to_broadcast([P, P]), identity16[:],
                                                start=True, stop=True)
                    last.then_inc(product_done, 1)
            SPREADS = N_PRODUCT * TILES // 4

            def look_up_products(m, first):
                for n in range(N_PRODUCT):
                    pe.wait_ge(one_hot_ready, m * N_PRODUCT + n + 1)
                    if first:
                        pe.wait_ge(table_split, n + 1)
                        if n < 2:
                            pe.wait_ge(ids_spread, SPREADS - 1 + n)
                    if not first or n >= 2:
                        pe.wait_ge(product_copied, m * N_PRODUCT + n - 1)
                    out = looked_up[n % 2][:, 0:COLS]
                    for part in range(PARTS):
                        for c in range(CHUNKS):
                            k = P if c < FULL else REST
                            last = nc.tensor.matmul(out, parts[0:k, n, part, c, :], one_hot[0:k, n % 2, c, :],
                                                    start=(part == 0 and c == 0),
                                                    stop=(part == PARTS - 1 and c == CHUNKS - 1))
                    last.then_inc(product_done, 1)

            def turn_tile(m, u, first):
                for g, slots in enumerate(GROUPS):
                    i = u * N_GROUPS + g
                    if g == 0:
                        pe.wait_ge(dense_loaded[u], (m + 1) * 16)
                    pe.wait_ge(gathered[u][g], (m + 1) * 16 * (len(slots) - (g == 0)))
                    if not first or i >= 2:
                        pe.wait_ge(turned_copied[i % 2], m * EVEN_TURNS + i // 2)
                    for q, slot in enumerate(slots):
                        last = nc.tensor.transpose(turned[i % 2][:, q * P:(q + 1) * P], rows[:, u, slot, :], identity[:])
                    last.then_inc(turned_done, 1)

            def dot_tile(m, u, first):
                for i in range(2):
                    pe.wait_ge(turned_copied[i], m * EVEN_TURNS + (u + 1) * N_GROUPS // 2)
                pe.wait_ge(product_copied, (m + 1) * N_PRODUCT)
                if first:
                    pe.wait_ge(padding_ready, 1)
                for b in range(FILLS):
                    i = u * FILLS + b
                    if not first or i >= 2:
                        pe.wait_ge(dots_copied, m * DOT_FILLS + i - 1)
                    for q in range(PER_BANK):
                        at = (b * PER_BANK + q) * IN_QUAD
                        last = nc.tensor.matmul(
                            dot_bank[b % 2][:, q * SQUARE:(q + 1) * SQUARE].rearrange("p (j g) -> p j g", j=IN_QUAD),
                            combined[:, u, at:at + IN_QUAD, :].rearrange("p j s -> p (j s)"),
                            combined[:, u, at:at + IN_QUAD, 0:VECTORS], start=True, stop=True)
                    last.then_inc(dots_done, 1)

            def layer1(m, first):
                pe.wait_ge(hidden_loaded, (m + 1) * HIDDEN_LOADS * 16)
                if first:
                    pe.wait_ge(weights_loaded, 7 * 16)
                    pe.wait_ge(weights_folded, 1)
                for n in range(LAYER1):
                    if not first or n >= 2:
                        pe.wait_ge(layer_copied, m * LAYERS + max(0, n - 1))
                    for k in range(K_TILES):
                        rows_k = P if k == 0 else K_PAIRS
                        last = nc.tensor.matmul(mlp_bank[n % 2][:, 0:COLS], w1[0:rows_k, k, n * P:(n + 1) * P],
                                                hidden0[0:rows_k, k, :], start=(k == 0), stop=(k == K_TILES - 1))
                    last.then_inc(layer_done, 1)

            def layer2(m):
                pe.wait_ge(layer_copied, m * LAYERS + LAYER1)
                for n in range(LAYER2):
                    for k in range(LAYER1):
                        last = nc.tensor.matmul(mlp_bank[n % 2][:, 0:COLS], w2[:, k, n * P:(n + 1) * P],
                                                hidden1[:, k, :], start=(k == 0), stop=(k == LAYER1 - 1))
                    last.then_inc(layer_done, 1)

            def layer3(m):
                pe.wait_ge(layer_copied, m * LAYERS + LAYER1 + LAYER2)
                for u in range(PER_BLOCK):
                    for k in range(LAYER2):
                        last = nc.tensor.matmul(mlp_bank[0][:, u:u + 1], hidden2[:, k, u, :], w3[:, k:k + 1],
                                                start=(k == 0), stop=(k == LAYER2 - 1))
                last.then_inc(layer_done, 1)

            look_up_products(0, True)
            turn_tile(0, 0, True)
            dot_tile(0, 0, True)
            turn_tile(0, 1, True)
            dot_tile(0, 1, True)

            def steady(m, first):
                look_up_products(m, False)
                layer1(m - 1, first)
                turn_tile(m, 0, False)
                layer2(m - 1)
                dot_tile(m, 0, False)
                layer3(m - 1)
                turn_tile(m, 1, False)
                dot_tile(m, 1, False)

            steady(1, True)
            with pe.Fori(2, BLOCKS) as m:
                steady(m, False)
            layer1(BLOCKS - 1, False)
            layer2(BLOCKS - 1)
            layer3(BLOCKS - 1)

        @block.scalar
        def _(act):
            for n in range(N_PRODUCT):
                for t in range(0, TILES, 4):
                    i = n * (TILES // 4) + t // 4
                    act.wait_ge(product_done, i + 1)
                    out = spread_ids[:, n, t // PER_BLOCK:t // PER_BLOCK + 2, :].rearrange("p m s -> p (m s)")
                    nc.scalar.copy(out, looked_up[i % 2][:, :]).then_inc(ids_spread, 1)
            SPREADS = N_PRODUCT * TILES // 4

            def copy_products(m):
                for n in range(N_PRODUCT):
                    act.wait_ge(product_done, SPREADS + m * N_PRODUCT + n + 1)
                    nc.scalar.copy(combined[:, :, :, PRODUCT_SLOT + n],
                                   looked_up[n % 2][:, 0:COLS].rearrange("d (u p) -> d u p", u=PER_BLOCK)
                                   ).then_inc(product_copied, 1)

            def copy_turned_odd(m, u):
                for g, slots in enumerate(GROUPS):
                    i = u * N_GROUPS + g
                    if i % 2 == 0:
                        continue
                    act.wait_ge(turned_done, m * TURNS + i + 1)
                    a, n = slots[0], len(slots)
                    nc.scalar.copy(combined[:, u, :, a:a + n],
                                   turned[1][:, 0:n * P].rearrange("d (s p) -> d p s", s=n)
                                   ).then_inc(turned_copied[1], 1)

            def copy_dots(m, u, first):
                if u == 0 and not first:
                    act.wait_ge(scratch_stored, m * SCRATCH_STORES * 16)
                    act.sem_inc(tile_may_start, 1)
                for b in range(FILLS):
                    act.wait_ge(dots_done, m * DOT_FILLS + u * FILLS + b + 1)
                    at = u * QUADS + b * PER_BANK
                    nc.scalar.copy(dots[:, :, at:at + PER_BANK],
                                   dot_bank[b % 2][:, 0:PER_BANK * SQUARE].rearrange("p (q c) -> p c q", q=PER_BANK)
                                   ).then_inc(dots_copied, 1)

            def steady(m, first):
                copy_products(m)
                copy_turned_odd(m, 0)
                copy_dots(m, 0, first)
                copy_turned_odd(m, 1)
                copy_dots(m, 1, first)

            steady(0, True)
            with act.Fori(1, BLOCKS) as m:
                steady(m, False)

        @block.vector
        def _(dve):
            dve.wait_ge(constants_ready, 2)
            nc.vector.tensor_copy(identity16[:], identity[:]).then_inc(ids16_ready, 1)
            dve.wait_ge(ids_loaded, 16)
            nc.vector.tensor_copy(ids16[:], all_ids[:]).then_inc(ids16_ready, 1)
            nc.vector.memset(combined[:, :, :, VECTORS:SLOTS], 0.0).then_inc(padding_ready, 1)

            def split_table(n):
                s = n % 2
                dve.wait_ge(table_loaded[s], (n // 2 + 1) * 32)
                for k, c in ((P, slice(0, FULL)), (REST, slice(FULL, CHUNKS))):
                    left = staged[0:k, s, c, :]
                    for part in range(PARTS):
                        to = parts[0:k, n, part, c, :]
                        last = nc.vector.tensor_copy(to, left)
                        if part == PARTS - 1:
                            break
                        last.then_inc(part_made, 1)
                        made[0] += 1
                        dve.wait_ge(part_made, made[0])
                        nc.vector.tensor_tensor(left, left, to, ALU.subtract).then_inc(part_made, 1)
                        made[0] += 1
                        dve.wait_ge(part_made, made[0])
                last.then_inc(table_split, 1)

            def make_one_hots(m, n, first):
                if first:
                    dve.wait_ge(ids_spread, (n + 1) * TILES // 4)
                if not first or n >= 2:
                    dve.wait_ge(product_done, N_PRODUCT * TILES // 4 + m * N_PRODUCT + n - 1)
                ids_of = spread_ids[:, n, bass.ds(m, 1), :].rearrange("p m s -> p (m s)")
                for c in range(CHUNKS):
                    last = nc.vector.tensor_scalar(one_hot[:, n % 2, c, :], ids_of, chunk_row[:, c:c + 1], None,
                                                   ALU.is_equal)
                last.then_inc(one_hot_ready, 1)

            def copy_turned_even(m, u):
                for g, slots in enumerate(GROUPS):
                    i = u * N_GROUPS + g
                    if i % 2:
                        continue
                    dve.wait_ge(turned_done, m * TURNS + i + 1)
                    a, n = slots[0], len(slots)
                    if g == 0:
                        nc.vector.tensor_copy(
                            hidden0[:, 0, :].rearrange("d (j u i) -> d u j i", j=IN_QUAD, u=PER_BLOCK)[:, u],
                            turned[0][:, 0:P].rearrange("d (i j) -> d j i", j=IN_QUAD))
                    nc.vector.tensor_copy(combined[:, u, :, a:a + n],
                                          turned[0][:, 0:n * P].rearrange("d (s p) -> d p s", s=n)
                                          ).then_inc(turned_copied[0], 1)

            def relu_layer1(m):
                relu_layer(m, 0, LAYER1, lambda n: hidden1[:, n, :], lambda out: out, bias1)

            def relu_layer2(m):
                relu_layer(m, LAYER1, LAYER2,
                           lambda n: hidden2[:, n, :, :].rearrange("h u (i j) -> h j u i", j=IN_QUAD),
                           lambda out: out.rearrange("h (j u i) -> h j u i", j=IN_QUAD, u=PER_BLOCK), bias2)

            def relu_layer(m, base, count, to, view, bias):
                for n in range(count):
                    dve.wait_ge(layer_done, m * LAYERS + base + n + 1)
                    nc.vector.tensor_scalar(to(n), view(mlp_bank[n % 2][:, 0:COLS]), bias[:, n:n + 1], 0.0,
                                            ALU.add, ALU.max).then_inc(layer_copied, 1)

            def copy_y(m):
                dve.wait_ge(layer_done, (m + 1) * LAYERS)
                nc.vector.tensor_copy(y_sb[:, bass.ds(m * PER_BLOCK, PER_BLOCK)],
                                      mlp_bank[0][:, 0:PER_BLOCK]).then_inc(layer_copied, 1)

            made = [0]
            for n in range(N_PRODUCT):
                split_table(n)
                make_one_hots(0, n, True)
            dve.wait_ge(weights_loaded, 7 * 16)
            nc.vector.tensor_tensor(w1[:, 0, :], w1[:, 0, :], w1_again[:], ALU.add).then_inc(weights_folded, 1)
            copy_turned_even(0, 0)
            copy_turned_even(0, 1)

            def steady(m):
                for n in range(N_PRODUCT):
                    make_one_hots(m, n, False)
                relu_layer1(m - 1)
                copy_turned_even(m, 0)
                relu_layer2(m - 1)
                copy_y(m - 1)
                copy_turned_even(m, 1)

            with dve.Fori(1, BLOCKS) as m:
                steady(m)
            relu_layer1(BLOCKS - 1)
            relu_layer2(BLOCKS - 1)
            copy_y(BLOCKS - 1)


_INS = (['r_dense_features', 'ids'] + [f'tbl_{i}' for i in range(FEATURES)]
        + ['W_top1', 'b_top1', 'W_top2', 'b_top2', 'W_top3'])


def kernel(**inputs):
    import concourse.bacc as bacc
    from concourse.bass_utils import run_bass_kernel_spmd as run

    nc = bacc.Bacc("TRN2", target_bir_lowering=False, num_devices=1)
    order = list(range(D)) + pair_rows() + list(range(D + PAIRS, D + PAIRS + D))
    arrays, args = {}, {}
    for name in _INS:
        a = np.asarray(inputs[name])
        if name == 'W_top1':
            a = a[np.array(order)]
        a = np.ascontiguousarray(a)
        arrays["in_" + name] = a
        args[name] = nc.dram_tensor("in_" + name, a.shape, mybir.dt.from_np(a.dtype), kind="ExternalInput").ap()
    y = nc.dram_tensor("out_y", (BATCH, 1), F32, kind="ExternalOutput").ap()
    build(nc, args['r_dense_features'], args['ids'], [args[f'tbl_{i}'] for i in range(FEATURES)],
          args['W_top1'], args['b_top1'], args['W_top2'], args['b_top2'], args['W_top3'], y)
    return run(nc, [arrays], core_ids=[0]).results[0]["out_y"]
```

```python
from contextlib import ExitStack

import numpy as np

import concourse.bass as bass
from concourse import mybir

F32, F32R, I32 = mybir.dt.float32, mybir.dt.float32r, mybir.dt.int32
ALU = mybir.AluOpType

P = 128
BATCH, D, FEATURES = 2048, 128, 26
TILES = BATCH // P
PER_BLOCK = 2
BLOCKS = TILES // PER_BLOCK
LAST = BLOCKS - 1
COLS = PER_BLOCK * P
VECTORS = FEATURES + 1
HALF = (VECTORS - 1) // 2
PAIRS = VECTORS * HALF
H1, H2 = 512, 256
LAYER1, LAYER2 = H1 // P, H2 // P
LAYERS = LAYER1 + LAYER2 + 1
FIRST_OUTS, LAST_OUTS = range(LAYER1 - 1), range(LAYER1 - 1, LAYER1)

PRODUCT_FEATURES = [1, 5, 7, 9, 17, 20, 22]
ROW_FEATURES = [f for f in range(FEATURES) if f not in PRODUCT_FEATURES]
N_ROW, N_PRODUCT = len(ROW_FEATURES), len(PRODUCT_FEATURES)
SLOT_VECTORS = [0] + [f + 1 for f in ROW_FEATURES] + [f + 1 for f in PRODUCT_FEATURES]
PRODUCT_SLOT = 1 + N_ROW
TABLE_ROWS = 1000
CHUNKS = -(-TABLE_ROWS // P)
ROWS_K = TABLE_ROWS // CHUNKS
ROWS_SPRAY = ROWS_K - ROWS_K % 16
HOT = 4
PARTS = 2
STAGES = 6
GROUPS = [list(range(a, min(a + 4, PRODUCT_SLOT))) for a in range(0, PRODUCT_SLOT, 4)]
N_GROUPS = len(GROUPS)
EVEN_GROUPS, ODD_GROUPS = (N_GROUPS + 1) // 2, N_GROUPS // 2
IN_QUAD = 4
QUADS = P // IN_QUAD
PER_BANK = 4
FILLS = QUADS // PER_BANK
SQUARE = IN_QUAD * VECTORS
WRAPPED = VECTORS + HALF
SPRAY = 32
WRAP_SPRAY = 16
MARGIN = SPRAY - VECTORS
F_PER_K = P // HALF
K_PAIRS = F_PER_K * HALF
K_TILES = 1 + PAIRS // K_PAIRS
SCRATCH_STORES = 2 * IN_QUAD
HIDDEN_LOADS = K_TILES - 1
WEIGHT_LOADS = 7


def pair_rows():
    at = {}
    for a in range(VECTORS):
        for b in range(a + 1, VECTORS):
            at[a, b] = D + len(at)
    rows = []
    for f in range(VECTORS):
        for k in range(1, HALF + 1):
            pair = SLOT_VECTORS[f], SLOT_VECTORS[(f + k) % VECTORS]
            rows.append(at[min(pair), max(pair)])
    return rows


def build(nc, dense, ids, ids_by_feature, tables, W1, b1, W2, b2, W3, y):
    with ExitStack() as ctx:
        def sb(name, shape, dt=F32):
            return ctx.enter_context(nc.sbuf_tensor(name, shape, dt))

        def sem(name):
            return ctx.enter_context(nc.semaphore(name))

        def bank(name):
            return ctx.enter_context(nc.psum_tensor(name, [P, 512], F32))

        all_ids = sb("all_ids", [P, TILES, FEATURES], I32)
        tile_ids = sb("tile_ids", [P, PER_BLOCK, FEATURES], I32)
        spread_ids = sb("spread_ids", [P, N_PRODUCT, COLS], I32)
        rows = sb("rows", [P, PER_BLOCK, PRODUCT_SLOT, D])
        parts = sb("parts", [P, N_PRODUCT, PARTS, CHUNKS, D], F32R)
        one_hot = sb("one_hot", [P, HOT, CHUNKS, COLS], F32R)
        chunk_row = sb("chunk_row", [P, CHUNKS])
        identity = sb("identity", [P, P])
        combined = sb("combined", [P, PER_BLOCK, P, VECTORS])
        ahead = sb("ahead", [P, N_PRODUCT, P])
        dots = sb("dots", [P, SQUARE, PER_BLOCK * QUADS])
        staged = dots[:].rearrange("p c s -> p (c s)")[:, 0:STAGES * CHUNKS * D].rearrange(
            "p (i c d) -> p i c d", i=STAGES, c=CHUNKS)
        hidden0 = sb("hidden0", [P, K_TILES, COLS])
        hidden1 = sb("hidden1", [P, LAYER1, COLS])
        hidden2 = sb("hidden2", [P, LAYER2, PER_BLOCK, P])
        w1 = sb("w1", [P, K_TILES, H1])
        w1_again = sb("w1_again", [P, H1])
        w2 = sb("w2", [P, LAYER1, H2])
        w3 = sb("w3", [P, LAYER2])
        bias1 = sb("bias1", [P, LAYER1])
        bias2 = sb("bias2", [P, LAYER2])
        y_sb = sb("y_sb", [P, TILES])
        scratch = nc.dram_tensor("scratch", (MARGIN + SPRAY, WRAPPED, IN_QUAD, PER_BLOCK * QUADS), F32).ap()

        turned = [bank(f"turned{i}") for i in range(2)]
        looked_up = [bank(f"looked_up{i}") for i in range(2)]
        group_bank = [turned[0], turned[1], looked_up[0], looked_up[1], turned[0]]
        dot_bank = [bank(f"dot_bank{i}") for i in range(2)]
        mlp_bank = [bank(f"mlp_bank{i}") for i in range(2)]

        ids_loaded = sem("ids_loaded")
        spread_loaded = sem("spread_loaded")
        weights_loaded = sem("weights_loaded")
        weights_folded = sem("weights_folded")
        table_loaded = [sem(f"table_loaded{n}") for n in range(N_PRODUCT)]
        high_part_made = sem("high_part_made")
        table_split = sem("table_split")
        identity_cleared = sem("identity_cleared")
        constants_ready = sem("constants_ready")
        tile_may_start = sem("tile_may_start")
        ids_copied = sem("ids_copied")
        tile_ids_ready = sem("tile_ids_ready")
        gathered = [[sem(f"gathered{u}_{g}") for g in range(N_GROUPS)] for u in range(PER_BLOCK)]
        dense_loaded = [sem(f"dense_loaded{u}") for u in range(PER_BLOCK)]
        one_hot_ready = sem("one_hot_ready")
        product_done = sem("product_done")
        product_copied = sem("product_copied")
        ahead_moved = sem("ahead_moved")
        turned_done = sem("turned_done")
        even_copied = sem("even_copied")
        odd_copied = sem("odd_copied")
        dense_kept = sem("dense_kept")
        dots_done = sem("dots_done")
        dots_copied = sem("dots_copied")
        dots_may_change = sem("dots_may_change")
        scratch_stored = sem("scratch_stored")
        hidden_loaded = sem("hidden_loaded")
        layer_done = sem("layer_done")
        layer_copied = sem("layer_copied")
        y_stored = sem("y_stored")

        block = ctx.enter_context(nc.Block())

        TURNS = PER_BLOCK * N_GROUPS
        DOT_FILLS = PER_BLOCK * FILLS

        ids_by_tile = ids.rearrange("(p t) f -> p t f", t=TILES)
        dense_by_tile = dense.rearrange("(p t) d -> p t d", t=TILES)

        def columns(ap, only):
            if only is None:
                return ap
            return ap.rearrange("k (j u i) -> k u j i", j=IN_QUAD, u=PER_BLOCK)[:, only]

        def tile_columns(ap, only):
            return ap[:, 0:COLS] if only is None else ap[:, 0:P]

        @block.sync
        def _(sp):
            def load_dense(m, u):
                sp.dma_start(rows[:, u, 0:1, :],
                             dense_by_tile[:, bass.ds(m * PER_BLOCK + u, 1), :]).then_inc(dense_loaded[u], 16)

            def load_spread_ids(m):
                sp.dma_start(spread_ids[:], ids_by_feature[bass.ds(m, 1), :, :].rearrange(
                    "m f s -> m (f s)").to_broadcast([P, N_PRODUCT * COLS]).rearrange(
                    "p (f s) -> p f s", f=N_PRODUCT)).then_inc(spread_loaded, 16)

            def load_table(n):
                t = tables[PRODUCT_FEATURES[n]]
                if n >= STAGES:
                    sp.wait_ge(table_split, n - STAGES + 1)
                t = t.rearrange("(p c) d -> p c d", c=CHUNKS)
                for a, b in ((0, ROWS_SPRAY), (ROWS_SPRAY, ROWS_K)):
                    sp.dma_start(staged[a:b, n % STAGES, :, :], t[a:b]).then_inc(table_loaded[n], 16)

            def next_spread_ids(m):
                sp.wait_ge(one_hot_ready, (m + 2) * N_PRODUCT)
                load_spread_ids(m + 2)

            def next_dense(m, u):
                sp.wait_ge(turned_done, m * TURNS + (u + 1) * N_GROUPS)
                load_dense(m + 1, u)

            def through_scratch(n, fills, first, only):
                s = slice(0, PER_BLOCK * QUADS) if only is None else slice(only * QUADS, (only + 1) * QUADS)
                sp.wait_ge(dots_copied, fills)
                if not first:
                    sp.wait_ge(hidden_loaded, n * HIDDEN_LOADS * 16)
                for j in range(IN_QUAD):
                    before = MARGIN if j == IN_QUAD - 1 else 0
                    a, r, c = VECTORS * j - before, MARGIN - before, VECTORS * j
                    sp.dma_start(scratch[r:r + SPRAY, 1:VECTORS, j, s],
                                 dots[a:a + SPRAY, c + 1:c + VECTORS, s]).then_inc(scratch_stored, 16)
                    a, r = VECTORS * (j + 1) - WRAP_SPRAY, MARGIN + VECTORS - WRAP_SPRAY
                    sp.dma_start(scratch[r:r + WRAP_SPRAY, VECTORS:WRAPPED, j, s],
                                 dots[a:a + WRAP_SPRAY, c:c + HALF, s]).then_inc(scratch_stored, 16)
                sp.wait_ge(scratch_stored, (n + 1) * SCRATCH_STORES * 16)
                if only is not None:
                    sp.wait_ge(layer_done, (n - 1) * LAYERS + LAYER1)
                for k in range(HIDDEN_LOADS):
                    step = WRAPPED + 1
                    at = MARGIN * WRAPPED + step * F_PER_K * k + 1
                    own = scratch.rearrange("f g j s -> (f g) j s")[at:at + step * F_PER_K, :, s]
                    if only is None:
                        own = own.rearrange("(f k) j s -> f k (j s)", k=step)[:, 0:HALF]
                        sp.dma_start(hidden0[0:K_PAIRS, 1 + k, :], own).then_inc(hidden_loaded, 16)
                    else:
                        to = hidden0[0:K_PAIRS, 1 + k, :].rearrange("p (j u i) -> p j u i", j=IN_QUAD, u=PER_BLOCK)
                        own = own.rearrange("(f k) j s -> f k j s", k=step)[:, 0:HALF]
                        sp.dma_start(to[:, :, only, :], own).then_inc(hidden_loaded, 16)

            sp.dma_start(all_ids[:], ids_by_tile).then_inc(ids_loaded, 16)
            load_spread_ids(0)
            load_table(0)
            load_table(1)
            load_dense(0, 0)
            for n in range(2, N_PRODUCT):
                load_table(n)
            sp.wait_ge(one_hot_ready, N_PRODUCT)
            load_spread_ids(1)
            load_dense(0, 1)
            sp.dma_start(w1[:, 0, :], W1[0:D, :]).then_inc(weights_loaded, 16)
            sp.dma_start(w1_again[:, :], W1[D + PAIRS:D + PAIRS + D, :]).then_inc(weights_loaded, 16)
            sp.dma_start(w1[0:K_PAIRS, 1:K_TILES, :],
                         W1[D:D + PAIRS, :].rearrange("(k p) n -> p k n", p=K_PAIRS)).then_inc(weights_loaded, 16)
            sp.dma_start(w2[:], W2.rearrange("(k p) n -> p k n", p=P)).then_inc(weights_loaded, 16)
            with nc.allow_non_contiguous_dma(reason="a few hundred words of biases, once"):
                sp.dma_start(w3[:], W3.rearrange("(k p) o -> p (k o)", p=P)).then_inc(weights_loaded, 16)
                sp.dma_start(bias1[:], b1.rearrange("(k p) -> p k", p=P)).then_inc(weights_loaded, 16)
                sp.dma_start(bias2[:], b2.rearrange("(k p) -> p k", p=P)).then_inc(weights_loaded, 16)

            def steady(m, first):
                next_dense(m, 0)
                next_spread_ids(m)
                next_dense(m, 1)
                through_scratch(m, (m + 1) * DOT_FILLS, first, None)

            steady(0, True)
            with sp.Fori(1, BLOCKS - 2) as m:
                steady(m, False)
            next_dense(LAST - 1, 0)
            next_dense(LAST - 1, 1)
            through_scratch(LAST - 1, LAST * DOT_FILLS, False, None)
            through_scratch(LAST, LAST * DOT_FILLS + FILLS, False, 0)
            through_scratch(LAST + 1, BLOCKS * DOT_FILLS, False, 1)
            sp.wait_ge(layer_copied, (BLOCKS + 1) * LAYERS)
            sp.dma_start(y.rearrange("(p t) o -> p (t o)", t=TILES), y_sb[:]).then_inc(y_stored, 16)
            sp.wait_ge(y_stored, 16)

        @block.gpsimd
        def _(pool):
            def gather_tile(m, u, first):
                if not first:
                    pool.wait_ge(turned_done, (m - 1) * TURNS + (u + 1) * N_GROUPS)
                    pool.sem_inc(tile_may_start, 1)
                nc.gpsimd.tensor_copy(tile_ids[:, u, :], all_ids[:, bass.ds(m * PER_BLOCK + u, 1), :].rearrange(
                    "p t f -> p (t f)")).then_inc(ids_copied, 1)
                pool.wait_ge(ids_copied, m * PER_BLOCK + u + 1)
                pool.sem_inc(tile_ids_ready, 1)
                for g, slots in enumerate(GROUPS):
                    for slot in slots:
                        if slot == 0:
                            continue
                        f = ROW_FEATURES[slot - 1]
                        nc.gpsimd.indirect_dma_start(
                            rows[:, u, slot, :], None, tables[f][:, :],
                            bass.IndirectOffsetOnAxis(ap=tile_ids[:, u, f:f + 1], axis=0)).then_inc(gathered[u][g], 16)

            nc.gpsimd.memset(identity[:], 0.0).then_inc(identity_cleared, 1)
            nc.gpsimd.iota(chunk_row[:], pattern=[[1, CHUNKS]], base=0, channel_multiplier=CHUNKS,
                           allow_small_or_imprecise_dtypes=True).then_inc(constants_ready, 1)
            pool.wait_ge(identity_cleared, 1)
            nc.gpsimd.affine_select(out=identity[:], in_=identity[:], compare_op=ALU.not_equal, fill=1.0, base=0,
                                    pattern=[[-1, P]], channel_multiplier=1).then_inc(constants_ready, 1)
            pool.wait_ge(ids_loaded, 16)
            for u in range(PER_BLOCK):
                gather_tile(0, u, True)
            with pool.Fori(1, BLOCKS) as m:
                for u in range(PER_BLOCK):
                    gather_tile(m, u, False)

        @block.tensor
        def _(pe):
            def look_up_products(m, first):
                for n in range(N_PRODUCT):
                    pe.wait_ge(one_hot_ready, m * N_PRODUCT + n + 1)
                    if first:
                        pe.wait_ge(table_split, n + 1)
                    if n >= 2:
                        pe.wait_ge(product_copied, m * N_PRODUCT + n - 1)
                    for part in range(PARTS):
                        for c in range(CHUNKS):
                            last = nc.tensor.matmul(looked_up[n % 2][:, 0:COLS], parts[0:ROWS_K, n, part, c, :],
                                                    one_hot[0:ROWS_K, n % HOT, c, :],
                                                    start=(part == 0 and c == 0),
                                                    stop=(part == PARTS - 1 and c == CHUNKS - 1))
                    last.then_inc(product_done, 1)

            def turn_tile(m, u, products):
                pe.wait_ge(product_copied, products)
                pe.wait_ge(dense_loaded[u], (m + 1) * 16)
                for g, slots in enumerate(GROUPS):
                    pe.wait_ge(gathered[u][g], (m + 1) * 16 * (len(slots) - (g == 0)))
                    if g == 4:
                        pe.wait_ge(even_copied, (m * PER_BLOCK + u) * EVEN_GROUPS + 1)
                    for q, slot in enumerate(slots):
                        last = nc.tensor.transpose(group_bank[g][:, q * P:(q + 1) * P], rows[:, u, slot, :], identity[:])
                    last.then_inc(turned_done, 1)

            def dot_tile(m, u, first):
                pe.wait_ge(even_copied, (m * PER_BLOCK + u + 1) * EVEN_GROUPS)
                pe.wait_ge(odd_copied, (m * PER_BLOCK + u + 1) * ODD_GROUPS)
                if u == 0:
                    pe.wait_ge(product_copied, (m + 1) * N_PRODUCT)
                else:
                    pe.wait_ge(ahead_moved, m + 1)
                for b in range(FILLS):
                    i = u * FILLS + b
                    if not first or i >= 2:
                        pe.wait_ge(dots_copied, m * DOT_FILLS + i - 1)
                    for q in range(PER_BANK):
                        at = (b * PER_BANK + q) * IN_QUAD
                        quad = combined[:, u, at:at + IN_QUAD, :].rearrange("d j s -> d (j s)")
                        last = nc.tensor.matmul(dot_bank[b % 2][0:SQUARE, q * SQUARE:(q + 1) * SQUARE], quad, quad,
                                                start=True, stop=True)
                    last.then_inc(dots_done, 1)

            def layer1(n, first, only=None, outs=range(LAYER1)):
                pe.wait_ge(hidden_loaded, (n + 1) * HIDDEN_LOADS * 16)
                pe.wait_ge(dense_kept, n + 1 if only is None else BLOCKS)
                if first:
                    pe.wait_ge(weights_loaded, WEIGHT_LOADS * 16)
                    pe.wait_ge(weights_folded, 1)
                for o in outs:
                    if not first or o >= 2:
                        pe.wait_ge(layer_copied, n * LAYERS + max(0, o - 1))
                    out = tile_columns(mlp_bank[o % 2], only)
                    if only is not None:
                        out = out.rearrange("h (j i) -> h j i", j=IN_QUAD)
                    for k in range(K_TILES):
                        rows_k = P if k == 0 else K_PAIRS
                        last = nc.tensor.matmul(out, w1[0:rows_k, k, o * P:(o + 1) * P],
                                                columns(hidden0[0:rows_k, k, :], only),
                                                start=(k == 0), stop=(k == K_TILES - 1))
                    last.then_inc(layer_done, 1)

            def layer2(n, only=None):
                pe.wait_ge(layer_copied, n * LAYERS + LAYER1)
                for o in range(LAYER2):
                    for k in range(LAYER1):
                        last = nc.tensor.matmul(tile_columns(mlp_bank[o % 2], only), w2[:, k, o * P:(o + 1) * P],
                                                tile_columns(hidden1[:, k, :], only),
                                                start=(k == 0), stop=(k == LAYER1 - 1))
                    last.then_inc(layer_done, 1)

            def layer3(n, only=None):
                pe.wait_ge(layer_copied, n * LAYERS + LAYER1 + LAYER2)
                for u in (range(PER_BLOCK) if only is None else [only]):
                    for k in range(LAYER2):
                        last = nc.tensor.matmul(mlp_bank[0][:, u:u + 1], hidden2[:, k, u, :], w3[:, k:k + 1],
                                                start=(k == 0), stop=(k == LAYER2 - 1))
                last.then_inc(layer_done, 1)

            look_up_products(0, True)
            turn_tile(0, 0, N_PRODUCT)
            dot_tile(0, 0, True)
            look_up_products(1, False)
            turn_tile(0, 1, 2 * N_PRODUCT)
            dot_tile(0, 1, True)

            def steady(m, first):
                turn_tile(m, 0, (m + 1) * N_PRODUCT)
                if not first:
                    layer3(m - 2)
                dot_tile(m, 0, False)
                look_up_products(m + 1, False)
                layer1(m - 1, first, outs=FIRST_OUTS)
                turn_tile(m, 1, (m + 2) * N_PRODUCT)
                layer1(m - 1, first, outs=LAST_OUTS)
                dot_tile(m, 1, False)
                layer2(m - 1)

            steady(1, True)
            with pe.Fori(2, LAST) as m:
                steady(m, False)
            turn_tile(LAST, 0, BLOCKS * N_PRODUCT)
            layer3(LAST - 2)
            dot_tile(LAST, 0, False)
            layer1(LAST - 1, False, outs=FIRST_OUTS)
            turn_tile(LAST, 1, BLOCKS * N_PRODUCT)
            layer1(LAST - 1, False, outs=LAST_OUTS)
            dot_tile(LAST, 1, False)
            layer2(LAST - 1)
            layer3(LAST - 1)
            for u in range(PER_BLOCK):
                layer1(LAST + u, False, u)
                layer2(LAST + u, u)
                layer3(LAST + u, u)

        def group_views(u, g):
            slots = GROUPS[g]
            n = len(slots)
            return (combined[:, u, :, slots[0]:slots[0] + n],
                    group_bank[g][:, 0:n * P].rearrange("d (s p) -> d p s", s=n))

        @block.scalar
        def _(act):
            def copy_products(m, first):
                for n in range(N_PRODUCT):
                    act.wait_ge(product_done, m * N_PRODUCT + n + 1)
                    nc.scalar.copy(combined[:, 0, :, PRODUCT_SLOT + n], looked_up[n % 2][:, 0:P])
                    nc.scalar.copy(ahead[:, n, :], looked_up[n % 2][:, P:COLS]).then_inc(product_copied, 1)

            def move_ahead(m, products):
                act.wait_ge(product_copied, products)
                act.sem_inc(dots_may_change, 1)
                nc.scalar.copy(combined[:, 1, :, PRODUCT_SLOT:VECTORS],
                               ahead[:].rearrange("d n p -> d p n")).then_inc(ahead_moved, 1)

            def copy_turned(m, u):
                for g in range(1, N_GROUPS, 2):
                    act.wait_ge(turned_done, m * TURNS + u * N_GROUPS + g + 1)
                    to, of = group_views(u, g)
                    nc.scalar.copy(to, of).then_inc(odd_copied, 1)

            def copy_dots(m, u, first):
                if u == 0 and not first:
                    act.wait_ge(scratch_stored, m * SCRATCH_STORES * 16)
                    act.sem_inc(dots_may_change, 1)
                for b in range(FILLS):
                    act.wait_ge(dots_done, m * DOT_FILLS + u * FILLS + b + 1)
                    at = u * QUADS + b * PER_BANK
                    nc.scalar.copy(dots[0:SQUARE, :, at:at + PER_BANK],
                                   dot_bank[b % 2][0:SQUARE, 0:PER_BANK * SQUARE].rearrange(
                                       "p (q c) -> p c q", q=PER_BANK)).then_inc(dots_copied, 1)

            for n in range(N_PRODUCT):
                act.wait_ge(table_loaded[n], 32)
                nc.scalar.copy(parts[0:ROWS_K, n, 0, :, :], staged[0:ROWS_K, n % STAGES, :, :]).then_inc(high_part_made, 1)
            copy_products(0, True)
            move_ahead(0, N_PRODUCT)
            copy_turned(0, 0)
            act.wait_ge(table_split, N_PRODUCT)
            copy_dots(0, 0, True)
            copy_products(1, False)
            copy_turned(0, 1)
            copy_dots(0, 1, True)
            move_ahead(1, 2 * N_PRODUCT)

            def steady(m):
                copy_turned(m, 0)
                copy_dots(m, 0, False)
                copy_products(m + 1, False)
                copy_turned(m, 1)
                copy_dots(m, 1, False)
                move_ahead(m + 1, (m + 2) * N_PRODUCT)

            with act.Fori(1, LAST) as m:
                steady(m)
            for u in range(PER_BLOCK):
                copy_turned(LAST, u)
                copy_dots(LAST, u, False)

        @block.vector
        def _(dve):
            def make_low_part(n):
                dve.wait_ge(table_loaded[n], 32)
                dve.wait_ge(high_part_made, n + 1)
                nc.vector.tensor_tensor(parts[0:ROWS_K, n, 1, :, :], staged[0:ROWS_K, n % STAGES, :, :],
                                        parts[0:ROWS_K, n, 0, :, :], ALU.subtract).then_inc(table_split, 1)

            def make_one_hots(m, n, first):
                if n == 0:
                    dve.wait_ge(spread_loaded, (m + 1) * 16)
                if n >= HOT:
                    dve.wait_ge(product_done, m * N_PRODUCT + n - HOT + 1)
                elif not first:
                    dve.wait_ge(product_done, m * N_PRODUCT)
                for c in range(CHUNKS):
                    last = nc.vector.tensor_scalar(one_hot[:, n % HOT, c, :], spread_ids[:, n, :],
                                                   chunk_row[:, c:c + 1], None, ALU.is_equal)
                last.then_inc(one_hot_ready, 1)

            def copy_turned(m, u, first=False):
                if u == 0 and not first:
                    dve.wait_ge(dense_kept, m)
                for g in range(0, N_GROUPS, 2):
                    dve.wait_ge(turned_done, m * TURNS + u * N_GROUPS + g + 1)
                    to, of = group_views(u, g)
                    nc.vector.tensor_copy(to, of).then_inc(even_copied, 1)

            def keep_dense(m, first):
                dve.wait_ge(even_copied, (m * PER_BLOCK + 1) * EVEN_GROUPS + 1)
                if not first:
                    dve.wait_ge(layer_done, (m - 1) * LAYERS + LAYER1)
                for u in range(PER_BLOCK):
                    last = nc.vector.tensor_copy(columns(hidden0[:, 0, :], u),
                                                 combined[:, u, :, 0].rearrange("d (i j) -> d j i", j=IN_QUAD))
                last.then_inc(dense_kept, 1)

            def relu_layer1(n, only=None, outs=range(LAYER1)):
                for o in outs:
                    dve.wait_ge(layer_done, n * LAYERS + o + 1)
                    nc.vector.tensor_scalar(tile_columns(hidden1[:, o, :], only), tile_columns(mlp_bank[o % 2], only),
                                            bias1[:, o:o + 1], 0.0, ALU.add, ALU.max).then_inc(layer_copied, 1)

            def relu_layer2(n, only=None):
                for o in range(LAYER2):
                    dve.wait_ge(layer_done, n * LAYERS + LAYER1 + o + 1)
                    of = tile_columns(mlp_bank[o % 2], only)
                    to = hidden2[:, o, :, :].rearrange("h u (i j) -> h j u i", j=IN_QUAD)
                    if only is None:
                        of = of.rearrange("h (j u i) -> h j u i", j=IN_QUAD, u=PER_BLOCK)
                    else:
                        of, to = of.rearrange("h (j i) -> h j i", j=IN_QUAD), to[:, :, only, :]
                    nc.vector.tensor_scalar(to, of, bias2[:, o:o + 1], 0.0, ALU.add, ALU.max).then_inc(layer_copied, 1)

            def copy_y(n, only=None):
                dve.wait_ge(layer_done, (n + 1) * LAYERS)
                if only is None:
                    to, of = y_sb[:, bass.ds(n * PER_BLOCK, PER_BLOCK)], mlp_bank[0][:, 0:PER_BLOCK]
                else:
                    t = LAST * PER_BLOCK + only
                    to, of = y_sb[:, t:t + 1], mlp_bank[0][:, only:only + 1]
                nc.vector.tensor_copy(to, of).then_inc(layer_copied, 1)

            dve.wait_ge(constants_ready, 2)
            for n in range(N_PRODUCT):
                make_one_hots(0, n, True)
                make_low_part(n)
            copy_turned(0, 0, True)
            for n in range(N_PRODUCT):
                make_one_hots(1, n, False)
            copy_turned(0, 1)
            keep_dense(0, True)
            dve.wait_ge(weights_loaded, WEIGHT_LOADS * 16)
            nc.vector.tensor_tensor(w1[:, 0, :], w1[:, 0, :], w1_again[:], ALU.add).then_inc(weights_folded, 1)

            def steady(m, first):
                copy_turned(m, 0)
                if not first:
                    copy_y(m - 2)
                for n in range(N_PRODUCT):
                    make_one_hots(m + 1, n, False)
                relu_layer1(m - 1, outs=FIRST_OUTS)
                copy_turned(m, 1)
                relu_layer1(m - 1, outs=LAST_OUTS)
                keep_dense(m, False)
                relu_layer2(m - 1)

            steady(1, True)
            with dve.Fori(2, LAST) as m:
                steady(m, False)
            copy_turned(LAST, 0)
            copy_y(LAST - 2)
            relu_layer1(LAST - 1, outs=FIRST_OUTS)
            copy_turned(LAST, 1)
            relu_layer1(LAST - 1, outs=LAST_OUTS)
            keep_dense(LAST, False)
            relu_layer2(LAST - 1)
            copy_y(LAST - 1)
            for u in range(PER_BLOCK):
                relu_layer1(LAST + u, u)
                relu_layer2(LAST + u, u)
                copy_y(LAST + u, u)


_INS = (['r_dense_features', 'ids'] + [f'tbl_{i}' for i in range(FEATURES)]
        + ['W_top1', 'b_top1', 'W_top2', 'b_top2', 'W_top3'])


def kernel(**inputs):
    import concourse.bacc as bacc
    from concourse.bass_utils import run_bass_kernel_spmd as run

    nc = bacc.Bacc("TRN2", target_bir_lowering=False, num_devices=1)
    order = list(range(D)) + pair_rows() + list(range(D + PAIRS, D + PAIRS + D))
    arrays, args = {}, {}
    for name in _INS:
        a = np.asarray(inputs[name])
        if name == 'W_top1':
            a = a[np.array(order)]
        a = np.ascontiguousarray(a)
        arrays["in_" + name] = a
        args[name] = nc.dram_tensor("in_" + name, a.shape, mybir.dt.from_np(a.dtype), kind="ExternalInput").ap()
    a = np.asarray(inputs['ids'])[:, PRODUCT_FEATURES].reshape(P, BLOCKS, PER_BLOCK, N_PRODUCT)
    a = np.ascontiguousarray(a.transpose(1, 3, 2, 0).reshape(BLOCKS, N_PRODUCT, COLS))
    arrays["in_ids_by_feature"] = a
    by_feature = nc.dram_tensor("in_ids_by_feature", a.shape, mybir.dt.from_np(a.dtype), kind="ExternalInput").ap()
    y = nc.dram_tensor("out_y", (BATCH, 1), F32, kind="ExternalOutput").ap()
    build(nc, args['r_dense_features'], args['ids'], by_feature, [args[f'tbl_{i}'] for i in range(FEATURES)],
          args['W_top1'], args['b_top1'], args['W_top2'], args['b_top2'], args['W_top3'], y)
    return run(nc, [arrays], core_ids=[0]).results[0]["out_y"]
```

```python
from contextlib import ExitStack

import numpy as np

import concourse.bass as bass
from concourse import mybir

F32, F32R, I32 = mybir.dt.float32, mybir.dt.float32r, mybir.dt.int32
ALU = mybir.AluOpType

P = 128
BATCH, D, FEATURES = 2048, 128, 26
TILES = BATCH // P
PER_BLOCK = 2
BLOCKS = TILES // PER_BLOCK
LAST = BLOCKS - 1
COLS = PER_BLOCK * P
VECTORS = FEATURES + 1
HALF = (VECTORS - 1) // 2
PAIRS = VECTORS * HALF
H1, H2 = 512, 256
LAYER1, LAYER2 = H1 // P, H2 // P
LAYERS = LAYER1 + LAYER2 + 1
BOTH = list(range(PER_BLOCK))
FIRST_OUTS, LAST_OUTS = range(1), range(1, LAYER1)

PRODUCT_FEATURES = [1, 5, 7, 9, 17, 20, 22, 24]
ROW_FEATURES = [f for f in range(FEATURES) if f not in PRODUCT_FEATURES]
N_ROW, N_PRODUCT = len(ROW_FEATURES), len(PRODUCT_FEATURES)
SLOT_VECTORS = [0] + [f + 1 for f in ROW_FEATURES] + [f + 1 for f in PRODUCT_FEATURES]
PRODUCT_SLOT = 1 + N_ROW
TABLE_ROWS = 1000
CHUNKS = -(-TABLE_ROWS // P)
ROWS_K = TABLE_ROWS // CHUNKS
ROWS_SPRAY = ROWS_K - ROWS_K % 16
HOT = 3
HIGH, LOW = range(2)
SPREAD = 2
SPREADS = N_PRODUCT // SPREAD
SPREAD_PLACES = 2
FIRST_IDS = [(0, 1), (1, N_PRODUCT)]
PART_PAIRS = [(HIGH, HIGH), (HIGH, LOW), (LOW, HIGH)]
GROUPS = [list(range(a, min(a + 4, PRODUCT_SLOT))) for a in range(0, PRODUCT_SLOT, 4)]
N_GROUPS = len(GROUPS)
EVEN_GROUPS, ODD_GROUPS = (N_GROUPS + 1) // 2, N_GROUPS // 2
IN_QUAD = 4
QUADS = P // IN_QUAD
PER_BANK = 4
FILLS = QUADS // PER_BANK
DOT_BANKS = 3
SQUARE = IN_QUAD * VECTORS
WRAPPED = VECTORS + HALF
SPRAY = 32
WRAP_SPRAY = 16
MARGIN = SPRAY - VECTORS
F_PER_K = P // HALF
K_PAIRS = F_PER_K * HALF
K_TILES = 1 + PAIRS // K_PAIRS
SCRATCH_STORES = 2 * IN_QUAD
HIDDEN_LOADS = K_TILES - 1
WEIGHT_LOADS = 7
WEIGHT_SPLITS = 3
SPLIT_AFTER = 5


def pair_rows():
    at = {}
    for a in range(VECTORS):
        for b in range(a + 1, VECTORS):
            at[a, b] = D + len(at)
    rows = []
    for f in range(VECTORS):
        for k in range(1, HALF + 1):
            pair = SLOT_VECTORS[f], SLOT_VECTORS[(f + k) % VECTORS]
            rows.append(at[min(pair), max(pair)])
    return rows


def build(nc, dense, ids, ids_by_feature, tables, W1, b1, W2, b2, W3, y):
    with ExitStack() as ctx:
        def sb(name, shape, dt=F32):
            return ctx.enter_context(nc.sbuf_tensor(name, shape, dt))

        def sb_split(name, shape):
            with nc.sbuf_tensor("whole_" + name, shape, F32) as whole:
                pass
            low = sb("low_" + name, shape, F32R)
            return whole, [sb("high_" + name, shape, F32R), low]

        def sem(name):
            return ctx.enter_context(nc.semaphore(name))

        def bank(name):
            return ctx.enter_context(nc.psum_tensor(name, [P, 512], F32))

        all_ids = sb("all_ids", [P, TILES, N_ROW], I32)
        tile_ids = sb("tile_ids", [P, PER_BLOCK, N_ROW], I32)
        spread_ids = sb("spread_ids", [P, SPREAD_PLACES, SPREAD, COLS], I32)
        rows = sb("rows", [P, PER_BLOCK, PRODUCT_SLOT, D])
        whole_tables, parts = sb_split("tables", [P, N_PRODUCT, CHUNKS, D])
        one_hot = sb("one_hot", [P, HOT, CHUNKS, COLS], F32R)
        chunk_row = sb("chunk_row", [P, CHUNKS])
        identity = sb("identity", [P, P])
        combined = sb("combined", [P, PER_BLOCK, P, VECTORS])
        with nc.sbuf_tensor("high_hidden1", [P, LAYER1, COLS], F32R) as high_hidden1:
            pass
        ahead = sb("ahead", [P, N_PRODUCT, P])
        with nc.sbuf_tensor("first_ids", [P, N_PRODUCT, COLS], I32) as first_ids:
            pass
        dots = sb("dots", [P, SQUARE, PER_BLOCK * QUADS])
        with nc.sbuf_tensor("whole_hidden0", [P, K_TILES, COLS], F32) as whole0:
            pass
        low_hidden0 = sb("low_hidden0", [P, K_TILES, COLS], F32R)
        high_dense = sb("high_dense", [P, COLS], F32R)
        with nc.sbuf_tensor("hidden2", [P, LAYER2, PER_BLOCK, P], F32) as hidden2:
            pass
        high_pairs = sb("high_pairs", [P, HIDDEN_LOADS, COLS], F32R)

        def hidden0(part, rows_k, k):
            if part == LOW:
                return low_hidden0[0:rows_k, k, :]
            return high_dense[:] if k == 0 else high_pairs[0:rows_k, k - 1, :]

        with nc.sbuf_tensor("whole_hidden1", [P, LAYER1, COLS], F32) as whole1:
            pass
        hidden1 = [high_hidden1, sb("low_hidden1", [P, LAYER1, COLS], F32R)]
        whole_w1, w1 = sb_split("w1", [P, K_TILES, H1])
        whole_w2, w2 = sb_split("w2", [P, LAYER1, H2])
        w3 = sb("w3", [P, LAYER2])
        bias1 = sb("bias1", [P, LAYER1])
        bias2 = sb("bias2", [P, LAYER2])
        y_sb = sb("y_sb", [P, TILES])
        w1_again = whole1[:].rearrange("p k s -> p (k s)")[:, 0:H1]
        scratch = nc.dram_tensor("scratch", (MARGIN + SPRAY, WRAPPED, IN_QUAD, PER_BLOCK * QUADS), F32).ap()

        turned = [bank(f"turned{i}") for i in range(2)]
        looked_up = [bank(f"looked_up{i}") for i in range(2)]
        dot_bank = [bank("dot_bank0"), bank("dot_bank1"), turned[1]]
        group_bank = [turned[0], turned[1], looked_up[0], looked_up[1], dot_bank[0]]
        mlp_bank = [bank(f"mlp_bank{i}") for i in range(2)]

        last_bank = looked_up + dot_bank[0:2]

        ids_loaded = sem("ids_loaded")
        first_ids_loaded = [sem(f"first_ids_loaded{i}") for i in range(len(FIRST_IDS))]
        spread_loaded = [sem(f"spread_loaded{i}") for i in range(SPREAD_PLACES)]
        weights_loaded = sem("weights_loaded")
        weights_folded = sem("weights_folded")
        weights_high = sem("weights_high")
        weights_split = sem("weights_split")
        pairs_may_split = sem("pairs_may_split")
        pairs_high = sem("pairs_high")
        pairs_split = sem("pairs_split")
        hidden1_may_split = sem("hidden1_may_split")
        hidden1_high = sem("hidden1_high")
        hidden1_split = sem("hidden1_split")
        dense_high = sem("dense_high")
        table_loaded = [sem(f"table_loaded{n}") for n in range(N_PRODUCT)]
        high_part_made = sem("high_part_made")
        table_split = sem("table_split")
        identity_cleared = sem("identity_cleared")
        constants_ready = sem("constants_ready")
        tile_may_start = sem("tile_may_start")
        first_tile_ids_ready = sem("first_tile_ids_ready")
        tile_ids_ready = sem("tile_ids_ready")
        gathered = [[sem(f"gathered{u}_{g}") for g in range(N_GROUPS)] for u in range(PER_BLOCK)]
        dense_loaded = [sem(f"dense_loaded{u}") for u in range(PER_BLOCK)]
        one_hot_ready = sem("one_hot_ready")
        half_used = sem("half_used")
        product_done = sem("product_done")
        product_copied = sem("product_copied")
        ahead_moved = sem("ahead_moved")
        turned_done = sem("turned_done")
        even_copied = sem("even_copied")
        odd_copied = sem("odd_copied")
        dense_kept = sem("dense_kept")
        dots_done = sem("dots_done")
        dots_copied = sem("dots_copied")
        dots_may_change = sem("dots_may_change")
        scratch_stored = sem("scratch_stored")
        hidden_loaded = [sem(f"hidden_loaded{k}") for k in range(HIDDEN_LOADS)]
        scratch_left = sem("scratch_left")
        layer_done = sem("layer_done")
        layer_copied = sem("layer_copied")
        y_stored = sem("y_stored")

        block = ctx.enter_context(nc.Block())

        TURNS = PER_BLOCK * N_GROUPS
        DOT_FILLS = PER_BLOCK * FILLS

        ids_by_tile = ids.rearrange("(p t) f -> p t f", t=TILES)
        dense_by_tile = dense.rearrange("(p t) d -> p t d", t=TILES)

        def tile_columns(ap, u):
            return ap.rearrange("k (j u i) -> k u j i", j=IN_QUAD, u=PER_BLOCK)[:, u]

        @block.sync
        def _(sp):
            def load_dense(m, u):
                sp.dma_start(rows[:, u, 0:1, :],
                             dense_by_tile[:, bass.ds(m * PER_BLOCK + u, 1), :]).then_inc(dense_loaded[u], 16)

            def load_spread_ids(m, q):
                i = q % SPREAD_PLACES
                sp.dma_start(spread_ids[:, i], ids_by_feature[bass.ds(m, 1), q * SPREAD:(q + 1) * SPREAD, :].rearrange(
                    "m f s -> m (f s)").to_broadcast([P, SPREAD * COLS]).rearrange(
                    "p (f s) -> p f s", f=SPREAD)).then_inc(spread_loaded[i], 16)

            def load_first_ids(i):
                a, b = FIRST_IDS[i]
                sp.dma_start(first_ids[:, a:b, :], ids_by_feature[0:1, a:b, :].rearrange(
                    "m f s -> m (f s)").to_broadcast([P, (b - a) * COLS]).rearrange(
                    "p (f s) -> p f s", f=b - a)).then_inc(first_ids_loaded[i], 16)

            def load_table(n):
                t = tables[PRODUCT_FEATURES[n]]
                t = t.rearrange("(p c) d -> p c d", c=CHUNKS)
                for a, b in ((0, ROWS_SPRAY), (ROWS_SPRAY, ROWS_K)):
                    sp.dma_start(whole_tables[a:b, n, :, :], t[a:b]).then_inc(table_loaded[n], 16)

            def next_spread_ids(m, spreads):
                for q in spreads:
                    sp.wait_ge(one_hot_ready, m * N_PRODUCT + (q - SPREAD_PLACES + 1) * SPREAD)
                    load_spread_ids(m + q // SPREADS, q % SPREADS)

            def next_dense(m, u):
                sp.wait_ge(turned_done, m * TURNS + (u + 1) * N_GROUPS)
                load_dense(m + 1, u)

            def store_dots(m, tiles, fills, first=False):
                s = slice(tiles[0] * QUADS, (tiles[-1] + 1) * QUADS)
                if not first:
                    for k in range(HIDDEN_LOADS):
                        sp.wait_ge(hidden_loaded[k], m * 16)
                        sp.sem_inc(scratch_left, 1)
                sp.wait_ge(dots_copied, fills)
                for j in range(IN_QUAD):
                    before = MARGIN if j == IN_QUAD - 1 else 0
                    a, r, c = VECTORS * j - before, MARGIN - before, VECTORS * j
                    sp.dma_start(scratch[r:r + SPRAY, 1:VECTORS, j, s],
                                 dots[a:a + SPRAY, c + 1:c + VECTORS, s]).then_inc(scratch_stored, 16)
                    a, r = VECTORS * (j + 1) - WRAP_SPRAY, MARGIN + VECTORS - WRAP_SPRAY
                    sp.dma_start(scratch[r:r + WRAP_SPRAY, VECTORS:WRAPPED, j, s],
                                 dots[a:a + WRAP_SPRAY, c:c + HALF, s]).then_inc(scratch_stored, 16)

            def load_pairs(m, stores, first=False):
                sp.wait_ge(scratch_stored, stores * 16)
                if not first:
                    sp.wait_ge(layer_done, (m - 1) * LAYERS + LAYER1)
                for k in range(HIDDEN_LOADS):
                    step = WRAPPED + 1
                    at = MARGIN * WRAPPED + step * F_PER_K * k + 1
                    own = scratch.rearrange("f g j s -> (f g) j s")[at:at + step * F_PER_K]
                    own = own.rearrange("(f k) j s -> f k (j s)", k=step)[:, 0:HALF]
                    sp.dma_start(whole0[0:K_PAIRS, 1 + k, :], own).then_inc(hidden_loaded[k], 16)

            sp.dma_start(all_ids[:], ids_by_tile).then_inc(ids_loaded, 16)
            load_first_ids(0)
            load_table(0)
            load_first_ids(1)
            for n in range(1, N_PRODUCT):
                load_table(n)
            load_dense(0, 0)
            for q in range(SPREAD_PLACES):
                load_spread_ids(1, q)
            load_dense(0, 1)
            sp.dma_start(whole_w1[:, 0, :], W1[0:D, :]).then_inc(weights_loaded, 16)
            sp.dma_start(w1_again, W1[D + PAIRS:D + PAIRS + D, :]).then_inc(weights_loaded, 16)
            sp.dma_start(whole_w1[0:K_PAIRS, 1:K_TILES, :],
                         W1[D:D + PAIRS, :].rearrange("(k p) n -> p k n", p=K_PAIRS)).then_inc(weights_loaded, 16)
            sp.dma_start(whole_w2[:], W2.rearrange("(k p) n -> p k n", p=P)).then_inc(weights_loaded, 16)
            with nc.allow_non_contiguous_dma(reason="a few hundred words of biases, once"):
                sp.dma_start(w3[:], W3.rearrange("(k p) o -> p (k o)", p=P)).then_inc(weights_loaded, 16)
                sp.dma_start(bias1[:], b1.rearrange("(k p) -> p k", p=P)).then_inc(weights_loaded, 16)
                sp.dma_start(bias2[:], b2.rearrange("(k p) -> p k", p=P)).then_inc(weights_loaded, 16)

            next_dense(0, 0)
            next_spread_ids(1, range(SPREAD_PLACES, HOT))
            next_dense(0, 1)
            next_spread_ids(1, range(HOT, SPREADS))
            store_dots(0, BOTH, DOT_FILLS, True)
            load_pairs(0, SCRATCH_STORES, True)
            next_spread_ids(1, range(SPREADS, SPREADS + SPREAD_PLACES))
            with sp.Fori(1, BLOCKS - 2) as m:
                next_dense(m, 0)
                next_spread_ids(m + 1, range(SPREAD_PLACES, SPREADS + SPREAD_PLACES))
                next_dense(m, 1)
                store_dots(m, BOTH, (m + 1) * DOT_FILLS)
                load_pairs(m, (m + 1) * SCRATCH_STORES)
            next_dense(LAST - 1, 0)
            next_spread_ids(LAST, range(SPREAD_PLACES, SPREADS))
            next_dense(LAST - 1, 1)
            store_dots(LAST - 1, BOTH, LAST * DOT_FILLS)
            load_pairs(LAST - 1, LAST * SCRATCH_STORES)
            store_dots(LAST, [0], LAST * DOT_FILLS + FILLS)
            store_dots(LAST, [1], BLOCKS * DOT_FILLS)
            load_pairs(LAST, (BLOCKS + 1) * SCRATCH_STORES)
            sp.wait_ge(layer_copied, BLOCKS * LAYERS)
            sp.dma_start(y.rearrange("(p t) o -> p (t o)", t=TILES), y_sb[:]).then_inc(y_stored, 16)
            sp.wait_ge(y_stored, 16)

        @block.gpsimd
        def _(pool):
            def gather_tile(m, u, first):
                if first:
                    nc.gpsimd.tensor_copy(tile_ids[:, u, :], all_ids[:, u, :]).then_inc(first_tile_ids_ready, 1)
                    pool.wait_ge(first_tile_ids_ready, u + 1)
                else:
                    pool.wait_ge(tile_ids_ready, (m - 1) * PER_BLOCK + u + 1)
                pool.sem_inc(tile_may_start, 1)
                for g, slots in enumerate(GROUPS):
                    for slot in slots:
                        if slot == 0:
                            continue
                        f = ROW_FEATURES[slot - 1]
                        nc.gpsimd.indirect_dma_start(
                            rows[:, u, slot, :], None, tables[f][:, :],
                            bass.IndirectOffsetOnAxis(ap=tile_ids[:, u, slot - 1:slot], axis=0)).then_inc(gathered[u][g], 16)

            nc.gpsimd.memset(identity[:], 0.0).then_inc(identity_cleared, 1)
            nc.gpsimd.iota(chunk_row[:], pattern=[[1, CHUNKS]], base=0, channel_multiplier=CHUNKS,
                           allow_small_or_imprecise_dtypes=True).then_inc(constants_ready, 1)
            pool.wait_ge(identity_cleared, 1)
            nc.gpsimd.affine_select(out=identity[:], in_=identity[:], compare_op=ALU.not_equal, fill=1.0, base=0,
                                    pattern=[[-1, P]], channel_multiplier=1).then_inc(constants_ready, 1)
            pool.wait_ge(ids_loaded, 16)
            for u in range(PER_BLOCK):
                gather_tile(0, u, True)
            with pool.Fori(1, BLOCKS) as m:
                for u in range(PER_BLOCK):
                    gather_tile(m, u, False)

        @block.tensor
        def _(pe):
            def look_up_products(m, first):
                for n in range(N_PRODUCT):
                    pe.wait_ge(one_hot_ready, m * N_PRODUCT + n + 1)
                    if first:
                        pe.wait_ge(table_split, n + 1)
                    if n >= 2:
                        pe.wait_ge(product_copied, m * N_PRODUCT + n - 1)
                    for c in range(CHUNKS):
                        for part in (HIGH, LOW):
                            last = nc.tensor.matmul(looked_up[n % 2][:, 0:COLS], parts[part][0:ROWS_K, n, c, :],
                                                    one_hot[0:ROWS_K, n % HOT, c, :],
                                                    start=(c == 0 and part == HIGH),
                                                    stop=(c == CHUNKS - 1 and part == LOW))
                        if c == CHUNKS // 2 - 1:
                            last.then_inc(half_used, 1)
                    last.then_inc(product_done, 1)

            def turn_tile(m, u, products, first=False):
                if not first:
                    pe.wait_ge(dots_copied, (m * PER_BLOCK + u) * FILLS)
                pe.wait_ge(dense_loaded[u], (m + 1) * 16)
                for g, slots in enumerate(GROUPS):
                    if g == 2:
                        pe.wait_ge(product_copied, products)
                    pe.wait_ge(gathered[u][g], (m + 1) * 16 * (len(slots) - (g == 0)))
                    for q, slot in enumerate(slots):
                        last = nc.tensor.transpose(group_bank[g][:, q * P:(q + 1) * P], rows[:, u, slot, :], identity[:])
                    last.then_inc(turned_done, 1)

            def dot_tile(m, u):
                pe.wait_ge(even_copied, (m * PER_BLOCK + u + 1) * EVEN_GROUPS)
                pe.wait_ge(odd_copied, (m * PER_BLOCK + u + 1) * ODD_GROUPS)
                if u == 0:
                    pe.wait_ge(product_copied, (m + 1) * N_PRODUCT)
                else:
                    pe.wait_ge(ahead_moved, m + 1)
                for b in range(FILLS):
                    if b >= DOT_BANKS:
                        pe.wait_ge(dots_copied, m * DOT_FILLS + u * FILLS + b - DOT_BANKS + 1)
                    for q in range(PER_BANK):
                        at = (b * PER_BANK + q) * IN_QUAD
                        quad = combined[:, u, at:at + IN_QUAD, :].rearrange("d j s -> d (j s)")
                        last = nc.tensor.matmul(dot_bank[b % DOT_BANKS][0:SQUARE, q * SQUARE:(q + 1) * SQUARE], quad, quad,
                                                start=True, stop=True)
                    last.then_inc(dots_done, 1)

            def layer1(n, first, outs=range(LAYER1)):
                pe.wait_ge(dense_kept, n + 1)
                if first:
                    pe.wait_ge(weights_split, WEIGHT_SPLITS)
                for o in outs:
                    if not first or o >= 2:
                        pe.wait_ge(layer_copied, n * LAYERS + max(0, o - 1))
                    for k in range(K_TILES):
                        if k > 0 and o == 0:
                            pe.wait_ge(pairs_split, n * HIDDEN_LOADS + k)
                        rows_k = P if k == 0 else K_PAIRS
                        for w, x in PART_PAIRS:
                            last = nc.tensor.matmul(mlp_bank[o % 2][:, 0:COLS], w1[w][0:rows_k, k, o * P:(o + 1) * P],
                                                    hidden0(x, rows_k, k), start=(k == 0 and w == x),
                                                    stop=(k == K_TILES - 1 and w == LOW))
                    last.then_inc(layer_done, 1)

            def last_layer1(tiles):
                if tiles[0] == 0:
                    pe.wait_ge(dense_kept, BLOCKS)
                    pe.wait_ge(dots_copied, BLOCKS * DOT_FILLS)
                for o in range(LAYER1):
                    for k in tiles:
                        if k > 0 and o == 0:
                            pe.wait_ge(pairs_split, LAST * HIDDEN_LOADS + k)
                        rows_k = P if k == 0 else K_PAIRS
                        for w, x in PART_PAIRS:
                            last = nc.tensor.matmul(last_bank[o][:, 0:COLS], w1[w][0:rows_k, k, o * P:(o + 1) * P],
                                                    hidden0(x, rows_k, k), start=(k == 0 and w == x),
                                                    stop=(k == K_TILES - 1 and w == LOW))
                    if tiles[-1] == K_TILES - 1:
                        last.then_inc(layer_done, 1)

            def layer2(n):
                pe.wait_ge(layer_copied, n * LAYERS + LAYER1 - 1)
                for o in range(LAYER2):
                    for k in range(LAYER1):
                        if o == 0:
                            pe.wait_ge(hidden1_split, n * LAYER1 + k + 1)
                        for w, x in PART_PAIRS:
                            last = nc.tensor.matmul(mlp_bank[o % 2][:, 0:COLS], w2[w][:, k, o * P:(o + 1) * P],
                                                    hidden1[x][:, k, :], start=(k == 0 and w == x),
                                                    stop=(k == LAYER1 - 1 and w == LOW))
                    last.then_inc(layer_done, 1)

            def layer3(n):
                pe.wait_ge(layer_copied, n * LAYERS + LAYER1 + LAYER2)
                for u in range(PER_BLOCK):
                    for k in range(LAYER2):
                        last = nc.tensor.matmul(mlp_bank[0][:, u:u + 1], hidden2[:, k, u, :], w3[:, k:k + 1],
                                                start=(k == 0), stop=(k == LAYER2 - 1))
                last.then_inc(layer_done, 1)

            look_up_products(0, True)
            turn_tile(0, 0, N_PRODUCT, True)
            dot_tile(0, 0)
            turn_tile(0, 1, N_PRODUCT)
            dot_tile(0, 1)
            look_up_products(1, False)

            def steady(m, first):
                turn_tile(m, 0, (m + 1) * N_PRODUCT)
                if not first:
                    layer2(m - 2)
                dot_tile(m, 0)
                if not first:
                    layer3(m - 2)
                look_up_products(m + 1, False)
                turn_tile(m, 1, (m + 2) * N_PRODUCT)
                layer1(m - 1, first, outs=FIRST_OUTS)
                dot_tile(m, 1)
                layer1(m - 1, first, outs=LAST_OUTS)

            steady(1, True)
            with pe.Fori(2, LAST) as m:
                steady(m, False)
            turn_tile(LAST, 0, BLOCKS * N_PRODUCT)
            layer2(LAST - 2)
            dot_tile(LAST, 0)
            layer3(LAST - 2)
            turn_tile(LAST, 1, BLOCKS * N_PRODUCT)
            layer1(LAST - 1, False, outs=FIRST_OUTS)
            dot_tile(LAST, 1)
            layer1(LAST - 1, False, outs=LAST_OUTS)
            layer2(LAST - 1)
            last_layer1([0])
            layer3(LAST - 1)
            last_layer1(list(range(1, K_TILES)))
            layer2(LAST)
            layer3(LAST)

        def group_views(u, g):
            slots = GROUPS[g]
            n = len(slots)
            return (combined[:, u, :, slots[0]:slots[0] + n],
                    group_bank[g][:, 0:n * P].rearrange("d (s p) -> d p s", s=n))

        @block.scalar
        def _(act):
            def copy_products(m, features=range(N_PRODUCT)):
                for n in features:
                    act.wait_ge(product_done, m * N_PRODUCT + n + 1)
                    nc.scalar.copy(combined[:, 0, :, PRODUCT_SLOT + n], looked_up[n % 2][:, 0:P])
                    nc.scalar.copy(ahead[:, n, :], looked_up[n % 2][:, P:COLS]).then_inc(product_copied, 1)

            def move_ahead(m, products):
                act.wait_ge(product_copied, products)
                act.sem_inc(dots_may_change, 1)
                nc.scalar.copy(combined[:, 1, :, PRODUCT_SLOT:VECTORS],
                               ahead[:].rearrange("d n p -> d p n")).then_inc(ahead_moved, 1)

            def copy_turned(m, u):
                for g in range(1, N_GROUPS, 2):
                    act.wait_ge(turned_done, m * TURNS + u * N_GROUPS + g + 1)
                    to, of = group_views(u, g)
                    nc.scalar.copy(to, of).then_inc(odd_copied, 1)

            def copy_dots(m, u, first):
                if u == 0 and not first:
                    act.wait_ge(scratch_stored, m * SCRATCH_STORES * 16)
                    act.sem_inc(dots_may_change, 1)
                for b in range(FILLS):
                    act.wait_ge(dots_done, m * DOT_FILLS + u * FILLS + b + 1)
                    at = u * QUADS + b * PER_BANK
                    nc.scalar.copy(dots[0:SQUARE, :, at:at + PER_BANK],
                                   dot_bank[b % DOT_BANKS][0:SQUARE, 0:PER_BANK * SQUARE].rearrange(
                                       "p (q c) -> p c q", q=PER_BANK)).then_inc(dots_copied, 1)

            def split_pairs(n, one_by_one=False):
                for k in range(HIDDEN_LOADS):
                    act.wait_ge(hidden_loaded[k], (n + 1) * 16)
                    if one_by_one:
                        high_pair_rows(k, k + 1)
                    else:
                        act.sem_inc(pairs_may_split, 1)
                if not one_by_one:
                    high_pair_rows(0, HIDDEN_LOADS)

            def high_pair_rows(a, b):
                nc.scalar.copy(high_pairs[0:K_PAIRS, a:b], whole0[0:K_PAIRS, 1 + a:1 + b, :]).then_inc(pairs_high, b - a)

            def split_hidden1(m, moved):
                act.wait_ge(ahead_moved, moved)
                act.sem_inc(hidden1_may_split, 1)
                for o in range(LAYER1):
                    if o == LAYER1 - 1:
                        act.wait_ge(layer_done, (m - 1) * LAYERS + LAYER1)
                        high_dense_parts()
                    high_output(m - 1, o)

            def high_output(n, o):
                act.wait_ge(layer_copied, n * LAYERS + o + 1)
                nc.scalar.copy(hidden1[HIGH][:, o, :], whole1[:, o, :]).then_inc(hidden1_high, 1)

            def high_dense_parts():
                for u in range(PER_BLOCK):
                    nc.scalar.copy(tile_columns(high_dense[:], u), combined[:, u, :, 0].rearrange(
                        "d (i j) -> d j i", j=IN_QUAD)).then_inc(dense_high, 1)

            def high_table(n):
                act.wait_ge(table_loaded[n], 32)
                nc.scalar.copy(parts[HIGH][0:ROWS_K, n, :, :], whole_tables[0:ROWS_K, n, :, :]).then_inc(high_part_made, 1)

            for n in range(HOT):
                high_table(n)
            for n in range(N_PRODUCT):
                copy_products(0, [n])
                if n + HOT < N_PRODUCT:
                    high_table(n + HOT)
            move_ahead(0, N_PRODUCT)
            copy_turned(0, 0)
            act.wait_ge(one_hot_ready, N_PRODUCT)
            copy_dots(0, 0, True)
            copy_turned(0, 1)
            act.wait_ge(even_copied, EVEN_GROUPS + 1)
            high_dense_parts()
            copy_dots(0, 1, True)
            copy_products(1, range(2))
            act.wait_ge(weights_loaded, WEIGHT_LOADS * 16)
            nc.scalar.copy(w2[HIGH][:], whole_w2[:]).then_inc(weights_high, 1)
            copy_products(1, range(2, 4))
            nc.scalar.copy(w1[HIGH][0:K_PAIRS, 1:K_TILES, :], whole_w1[0:K_PAIRS, 1:K_TILES, :]).then_inc(weights_high, 1)
            copy_products(1, range(4, 6))
            act.wait_ge(weights_folded, 1)
            nc.scalar.copy(w1[HIGH][:, 0, :], whole_w1[:, 0, :]).then_inc(weights_high, 1)
            copy_products(1, range(6, N_PRODUCT))
            move_ahead(1, 2 * N_PRODUCT)

            def steady(m):
                copy_turned(m, 0)
                copy_dots(m, 0, False)
                copy_products(m + 1, range(SPLIT_AFTER))
                split_pairs(m - 1)
                copy_products(m + 1, range(SPLIT_AFTER, N_PRODUCT))
                copy_turned(m, 1)
                copy_dots(m, 1, False)
                move_ahead(m + 1, (m + 2) * N_PRODUCT)
                split_hidden1(m, m + 2)

            with act.Fori(1, LAST) as m:
                steady(m)
            copy_turned(LAST, 0)
            copy_dots(LAST, 0, False)
            act.wait_ge(layer_done, (LAST - 1) * LAYERS)
            split_pairs(LAST - 1)
            copy_turned(LAST, 1)
            copy_dots(LAST, 1, False)
            split_hidden1(LAST, BLOCKS)
            act.wait_ge(layer_done, LAST * LAYERS)
            split_pairs(LAST, True)
            for o in range(LAYER1):
                high_output(LAST, o)

        @block.vector
        def _(dve):
            def make_low_part(n):
                dve.wait_ge(table_loaded[n], 32)
                dve.wait_ge(high_part_made, n + 1)
                nc.vector.tensor_tensor(parts[LOW][0:ROWS_K, n, :, :], whole_tables[0:ROWS_K, n, :, :],
                                        parts[HIGH][0:ROWS_K, n, :, :], ALU.subtract).then_inc(table_split, 1)

            def make_one_hots(m, n, first):
                q = n // SPREAD
                i = q % SPREAD_PLACES
                of = first_ids[:, n, :] if first else spread_ids[:, i, n % SPREAD, :]
                if first and n < len(FIRST_IDS):
                    dve.wait_ge(first_ids_loaded[n], 16)
                elif not first and n % SPREAD == 0:
                    dve.wait_ge(spread_loaded[i], ((m - 1) * (SPREADS // SPREAD_PLACES) + q // SPREAD_PLACES + 1) * 16)
                if n == 0 and not first:
                    dve.wait_ge(product_done, m * N_PRODUCT)
                for c in range(CHUNKS):
                    if n >= HOT and c == 0:
                        dve.wait_ge(half_used, m * N_PRODUCT + n - HOT + 1)
                    if n >= HOT and c == CHUNKS // 2:
                        dve.wait_ge(product_done, m * N_PRODUCT + n - HOT + 1)
                    last = nc.vector.tensor_scalar(one_hot[:, n % HOT, c, :], of,
                                                   chunk_row[:, c:c + 1], None, ALU.is_equal)
                last.then_inc(one_hot_ready, 1)

            def copy_turned(m, u, first=False):
                if u == 0 and not first:
                    dve.wait_ge(dense_kept, m)
                for g in range(0, N_GROUPS, 2):
                    dve.wait_ge(turned_done, m * TURNS + u * N_GROUPS + g + 1)
                    if g == N_GROUPS - 1 and m is not LAST:
                        nc.vector.tensor_copy(tile_ids[:, u, :], all_ids[:, bass.ds((m + 1) * PER_BLOCK + u, 1), :].rearrange(
                            "p t f -> p (t f)")).then_inc(tile_ids_ready, 1)
                    to, of = group_views(u, g)
                    nc.vector.tensor_copy(to, of).then_inc(even_copied, 1)

            def keep_dense(m, first):
                dve.wait_ge(even_copied, (m * PER_BLOCK + 1) * EVEN_GROUPS + 1)
                if not first:
                    dve.wait_ge(layer_done, (m - 1) * LAYERS + LAYER1)
                dve.wait_ge(dense_high, (m + 1) * PER_BLOCK)
                for u in range(PER_BLOCK):
                    last = nc.vector.tensor_tensor(tile_columns(low_hidden0[:, 0, :], u),
                                                   combined[:, u, :, 0].rearrange("d (i j) -> d j i", j=IN_QUAD),
                                                   tile_columns(high_dense[:], u), ALU.subtract)
                last.then_inc(dense_kept, 1)

            def low_pairs(n, one_by_one=False):
                for a, b in ([(k, k + 1) for k in range(HIDDEN_LOADS)] if one_by_one else [(0, HIDDEN_LOADS)]):
                    dve.wait_ge(pairs_high, n * HIDDEN_LOADS + b)
                    nc.vector.tensor_tensor(low_hidden0[0:K_PAIRS, 1 + a:1 + b, :], whole0[0:K_PAIRS, 1 + a:1 + b, :],
                                            high_pairs[0:K_PAIRS, a:b], ALU.subtract).then_inc(pairs_split, b - a)

            def low_hidden1(n, o):
                dve.wait_ge(hidden1_high, n * LAYER1 + o + 1)
                nc.vector.tensor_tensor(hidden1[LOW][:, o, :], whole1[:, o, :], hidden1[HIGH][:, o, :],
                                        ALU.subtract).then_inc(hidden1_split, 1)

            def relu_layer1(n, banks=2 * mlp_bank):
                for o in range(LAYER1):
                    dve.wait_ge(layer_done, n * LAYERS + o + 1)
                    nc.vector.tensor_scalar(whole1[:, o, :], banks[o][:, 0:COLS],
                                            bias1[:, o:o + 1], 0.0, ALU.add, ALU.max).then_inc(layer_copied, 1)
                    if o > 0:
                        low_hidden1(n, o - 1)

            def relu_layer2(n):
                for o in range(LAYER2):
                    dve.wait_ge(layer_done, n * LAYERS + LAYER1 + o + 1)
                    nc.vector.tensor_scalar(hidden2[:, o, :, :].rearrange("h u (i j) -> h j u i", j=IN_QUAD),
                                            mlp_bank[o % 2][:, 0:COLS].rearrange("h (j u i) -> h j u i", j=IN_QUAD, u=PER_BLOCK),
                                            bias2[:, o:o + 1], 0.0, ALU.add, ALU.max).then_inc(layer_copied, 1)

            def copy_y(n):
                dve.wait_ge(layer_done, (n + 1) * LAYERS)
                nc.vector.tensor_copy(y_sb[:, bass.ds(n * PER_BLOCK, PER_BLOCK)],
                                      mlp_bank[0][:, 0:PER_BLOCK]).then_inc(layer_copied, 1)

            dve.wait_ge(constants_ready, 2)
            dve.wait_ge(ids_loaded, 16)
            for n in range(N_PRODUCT):
                make_one_hots(0, n, True)
                make_low_part(n)
            copy_turned(0, 0, True)
            for n in range(HOT):
                make_one_hots(1, n, False)
            dve.wait_ge(weights_loaded, WEIGHT_LOADS * 16)
            nc.vector.tensor_tensor(whole_w1[:, 0, :], whole_w1[:, 0, :], w1_again, ALU.add).then_inc(weights_folded, 1)
            copy_turned(0, 1)
            keep_dense(0, True)
            for n in range(HOT, N_PRODUCT):
                make_one_hots(1, n, False)
            dve.wait_ge(weights_high, WEIGHT_SPLITS)
            nc.vector.tensor_tensor(w2[LOW][:], whole_w2[:], w2[HIGH][:], ALU.subtract).then_inc(weights_split, 1)
            nc.vector.tensor_tensor(w1[LOW][0:K_PAIRS, 1:K_TILES, :], whole_w1[0:K_PAIRS, 1:K_TILES, :],
                                    w1[HIGH][0:K_PAIRS, 1:K_TILES, :], ALU.subtract).then_inc(weights_split, 1)
            nc.vector.tensor_tensor(w1[LOW][:, 0, :], whole_w1[:, 0, :], w1[HIGH][:, 0, :],
                                    ALU.subtract).then_inc(weights_split, 1)

            def steady(m, first):
                copy_turned(m, 0)
                if not first:
                    relu_layer2(m - 2)
                for n in range(HOT):
                    make_one_hots(m + 1, n, False)
                if not first:
                    copy_y(m - 2)
                for n in range(HOT, N_PRODUCT):
                    make_one_hots(m + 1, n, False)
                low_pairs(m - 1)
                copy_turned(m, 1)
                relu_layer1(m - 1)
                keep_dense(m, False)
                low_hidden1(m - 1, LAYER1 - 1)

            steady(1, True)
            with dve.Fori(2, LAST) as m:
                steady(m, False)
            copy_turned(LAST, 0)
            relu_layer2(LAST - 2)
            copy_y(LAST - 2)
            low_pairs(LAST - 1)
            copy_turned(LAST, 1)
            relu_layer1(LAST - 1)
            low_hidden1(LAST - 1, LAYER1 - 1)
            keep_dense(LAST, False)
            relu_layer2(LAST - 1)
            copy_y(LAST - 1)
            low_pairs(LAST, True)
            relu_layer1(LAST, last_bank)
            low_hidden1(LAST, LAYER1 - 1)
            relu_layer2(LAST)
            copy_y(LAST)


_INS = (['r_dense_features', 'ids'] + [f'tbl_{i}' for i in range(FEATURES)]
        + ['W_top1', 'b_top1', 'W_top2', 'b_top2', 'W_top3'])


def kernel(**inputs):
    import concourse.bacc as bacc
    from concourse.bass_utils import run_bass_kernel_spmd as run

    nc = bacc.Bacc("TRN2", target_bir_lowering=False, num_devices=1)
    order = list(range(D)) + pair_rows() + list(range(D + PAIRS, D + PAIRS + D))
    arrays, args = {}, {}
    for name in _INS:
        a = np.asarray(inputs[name])
        if name == 'W_top1':
            a = a[np.array(order)]
        if name == 'ids':
            a = a[:, ROW_FEATURES]
        a = np.ascontiguousarray(a)
        arrays["in_" + name] = a
        args[name] = nc.dram_tensor("in_" + name, a.shape, mybir.dt.from_np(a.dtype), kind="ExternalInput").ap()
    a = np.asarray(inputs['ids'])[:, PRODUCT_FEATURES].reshape(P, BLOCKS, PER_BLOCK, N_PRODUCT)
    a = np.ascontiguousarray(a.transpose(1, 3, 2, 0).reshape(BLOCKS, N_PRODUCT, COLS))
    arrays["in_ids_by_feature"] = a
    by_feature = nc.dram_tensor("in_ids_by_feature", a.shape, mybir.dt.from_np(a.dtype), kind="ExternalInput").ap()
    y = nc.dram_tensor("out_y", (BATCH, 1), F32, kind="ExternalOutput").ap()
    build(nc, args['r_dense_features'], args['ids'], by_feature, [args[f'tbl_{i}'] for i in range(FEATURES)],
          args['W_top1'], args['b_top1'], args['W_top2'], args['b_top2'], args['W_top3'], y)
    return run(nc, [arrays], core_ids=[0]).results[0]["out_y"]
```
